# Optimizing a Trainium2 kernel written in Bass

```python
import numpy as np
import jax
import jax.numpy as jnp

def _softmax(x, axis=-1):
    return jax.nn.softmax(x, axis=axis)

def _gelu(x):
    return jax.nn.gelu(x, approximate=True)

def _silu(x):
    return jax.nn.silu(x)

def _sigmoid(x):
    return jax.nn.sigmoid(x)

def _layernorm(x, axis=-1, eps=1e-05):
    m = jnp.mean(x, axis=axis, keepdims=True)
    v = jnp.var(x, axis=axis, keepdims=True)
    return (x - m) / jnp.sqrt(v + eps)

def _scatter_add(tgt, idx, src, axis=0):
    return tgt.at[idx].add(src)

def _segment_sum(src, seg, n):
    return jax.ops.segment_sum(src, seg, n)
kernel_name = 'mk_sandwich_d1_jaxref_r4_050e3d'

def setup_inputs(seed: int=0):
    np.random.seed(seed)
    _w = jnp.asarray

    def _L0_attn_setup():
        import jax, jax.numpy as jnp
        import numpy as np
        H = 1024
        D = H // 4
        key = jax.random.key(seed)
        k1, k2, k3, k4, k5 = jax.random.split(key, 5)
        x = jax.random.normal(k1, (4, 1024, H), dtype=jnp.float32)
        s_in = 1.0 / np.sqrt(H)
        Wqkv = jax.random.normal(k2, (H, 3 * D), dtype=jnp.float32) * s_in
        bqkv = jax.random.normal(k3, (3 * D,), dtype=jnp.float32) * 0.01
        Wo = jax.random.normal(k4, (D, H), dtype=jnp.float32) * (1.0 / np.sqrt(D))
        bo = jax.random.normal(k5, (H,), dtype=jnp.float32) * 0.01
        return {'x': x, 'Wqkv': Wqkv, 'bqkv': bqkv, 'Wo': Wo, 'bo': bo}
    _L0_attn_in = _L0_attn_setup()

    def _L0_ffn_setup():
        import jax, jax.numpy as jnp
        import numpy as np
        D = 1024
        F = 2752
        B, S = (4, 512)
        key = jax.random.key(seed)
        k_x, k_g, k_u, k_d = jax.random.split(key, 4)
        scale = 0.02
        return {'x': jax.random.normal(k_x, (B, S, D), dtype=jnp.float32), 'W_gate': jax.random.normal(k_g, (F, D), dtype=jnp.float32) * scale, 'W_up': jax.random.normal(k_u, (F, D), dtype=jnp.float32) * scale, 'W_down': jax.random.normal(k_d, (D, F), dtype=jnp.float32) * scale}
    _L0_ffn_in = _L0_ffn_setup()
    _d = {'L0_attn_x': _L0_attn_in['x'], 'L0_attn_Wqkv': _L0_attn_in['Wqkv'], 'L0_attn_bqkv': _L0_attn_in['bqkv'], 'L0_attn_Wo': _L0_attn_in['Wo'], 'L0_attn_bo': _L0_attn_in['bo'], 'L0_ffn_W_gate': _L0_ffn_in['W_gate'], 'L0_ffn_W_up': _L0_ffn_in['W_up'], 'L0_ffn_W_down': _L0_ffn_in['W_down']}
    _x0 = _d['L0_attn_x']
    _d['L0_attn_x'] = jax.random.normal(jax.random.fold_in(jax.random.key(seed), 1), (1, 2048, 1024), dtype=_x0.dtype)
    del _x0
    return _d

def reference(L0_attn_x, L0_attn_Wqkv, L0_attn_bqkv, L0_attn_Wo, L0_attn_bo, L0_ffn_W_gate, L0_ffn_W_up, L0_ffn_W_down):

    def _L0_attn_ref(x, Wqkv, bqkv, Wo, bo):
        import jax, jax.numpy as jnp
        import numpy as np
        H = 1024
        D = H // 4
        B, S, C = x.shape
        d = C // 4
        qkv = jnp.einsum('bsc,cf->bsf', x, Wqkv) + bqkv
        qkv = qkv.reshape(B, S, 3, d)
        q, k, v = (qkv[:, :, 0], qkv[:, :, 1], qkv[:, :, 2])
        scale = 1.0 / jnp.sqrt(jnp.float32(d)).astype(x.dtype)
        attn = jnp.einsum('bqd,bkd->bqk', q, k) * scale
        attn = jax.nn.softmax(attn, axis=-1)
        out = jnp.einsum('bqk,bkd->bqd', attn, v)
        return jnp.einsum('bqd,dc->bqc', out, Wo) + bo

    def _L0_ffn_ref(x, W_gate, W_up, W_down):
        import jax, jax.numpy as jnp
        import numpy as np
        D = 1024
        F = 2752
        B, S = (4, 512)
        out_shape = x.shape[:-1] + (W_down.shape[0],)
        xt = x.reshape(-1, x.shape[-1])
        up = xt @ W_up.T
        gate = jax.nn.silu(xt @ W_gate.T)
        y = gate * up @ W_down.T
        return y.reshape(out_shape)
    x = L0_attn_x
    x = x + _layernorm(_L0_attn_ref(_layernorm(x, axis=-1), L0_attn_Wqkv, L0_attn_bqkv, L0_attn_Wo, L0_attn_bo), axis=-1)
    x = x + _layernorm(_L0_ffn_ref(_layernorm(x, axis=-1), L0_ffn_W_gate, L0_ffn_W_up, L0_ffn_W_down), axis=-1)
    return x

_drawn_inputs = setup_inputs


def setup_inputs(seed=0):
    import zlib

    import numpy as np

    out = dict(_drawn_inputs(seed))
    spreads = {}
    factors = {}
    for name, (base, spread) in spreads.items():
        noise = np.random.default_rng([zlib.crc32(name.encode()), seed]).standard_normal(out[name].shape)
        drawn = base * np.exp(spread * noise) if base else spread * noise
        out[name] = jnp.asarray(drawn.astype(out[name].dtype))
    for name, factor in factors.items():
        out[name] = (out[name] * factor).astype(out[name].dtype)
    return out
```

```python
import concourse.bass as bass
from concourse import mybir

F32 = mybir.dt.float32
F32R = mybir.dt.float32r
ACT = mybir.ActivationFunctionType
ALU = mybir.AluOpType
AX = mybir.AxisListType

P = 128
S = 2048
C = 1024
D = 256
F = 2752
EPS = 1e-5
BANK = 512
KC = C // P
KD = D // P
TILES = S // P
BLOCK = 512
TPB = BLOCK // P
BLOCKS = S // BLOCK
FULL = F // P
REST = F - FULL * P
HALF = C // BANK
ITEM = 2048
CPI = ITEM // BANK
DOWN = (FULL - 1) // CPI
UPS = FULL + 1
ITEMS = UPS + HALF * (DOWN + 1)
HIGH, LOW = 0, 1
assert 2 * REST == P and FULL == CPI * DOWN + 1 and ITEMS % 2 == 0


def transformer_block(nc, x, wqkv, bqk, bv, wo, bo, wffn, out):
    KB = 1024
    base = -(-nc.sbuf_base // 64) * 64

    def at(name, kb, shape, dt=F32):
        return nc.alloc_sbuf_tensor_at(name, [P] + shape, dt, offset=base + int(kb * KB))

    q_t = at("q_t", 0, [KD, S])
    k_t = at("k_t", 16, [KD, 2, S], F32R)
    v = at("v", 48, [TILES, 2, D], F32R)
    xn_t = at("xn_t", 80, [2, KC, BLOCK], F32R)
    wqkv_raw = at("wqkv_raw", 112, [2, KC // 2, 3 * D])
    x_tile = at("x_tile", 136, [TPB, C])
    v_half = at("v_half", 152, [D])
    v_sum = at("v_sum", 153, [2, D])
    bv_sb = at("bv_sb", 155, [D])
    wqk = at("wqk", 156, [2, KC, 2 * D], F32R)
    wv = at("wv", 188, [KC, 2, D], F32R)
    probs = at("probs", 80, [S])
    probs_t = at("probs_t", 88, [2, TILES, P], F32R)
    wo_sb = at("wo_sb", 104, [2, KD, C], F32R)
    wo_raw = at("wo_raw", 120, [KD, C])
    q_tile = at("q_tile", 128, [2, KD, P], F32R)
    o_half = at("o_half", 130, [D])
    o_sum = at("o_sum", 131, [D])
    o_t = at("o_t", 132, [2, KD, P], F32R)
    x1_tile = at("x1_tile", 134, [C])
    x_res = at("x_res", 138, [C])
    bo_sb = at("bo_sb", 142, [C])
    t_tile = at("t_tile", 0, [TPB, C])
    x1n_t = at("x1n_t", 16, [2, KC, BLOCK], F32R)
    h_t = at("h_t", 48, [FULL, 2, BLOCK], F32R)
    h_rest = at("h_rest", 48 + 4 * FULL, [BLOCK], F32R)
    y_tile = at("y_tile", 134, [TPB, C])
    silu_sb = at("silu_sb", 150, [2, BLOCK])
    h_f32 = at("h_f32", 154, [BLOCK])
    w_raw = at("w_raw", 156, [2, ITEM])
    w_sb = at("w_sb", 172, [2, 2, ITEM], F32R)
    ident = at("ident", 204, [P])
    small = [204.5]

    def tiny(name, shape):
        size = 4
        for n in shape:
            size *= n
        t = at(name, small[0], shape)
        small[0] += -(-size // 32) * 32 / KB
        return t

    bqk_sb = tiny("bqk_sb", [2 * KD])
    minus_half = tiny("minus_half", [1])
    eps = tiny("eps", [1])
    bank_max = tiny("bank_max", [4])
    row_max = tiny("row_max", [1])
    neg_max = tiny("neg_max", [1])
    bank_sum = tiny("bank_sum", [4])
    row_sum = tiny("row_sum", [1])
    inv_sum = tiny("inv_sum", [1])

    ps = nc.alloc_psum_tensor("ps", [P, 8, BANK], F32)
    x1_dram = nc.dram_tensor("x1_dram", [S, C], F32)

    sem = nc.alloc_semaphore

    class Norm:

        def __init__(self, name, places):
            self.places = places
            self.stats = tiny(name + "_stats", [places, 2, 6])
            self.moments = tiny(name + "_moments", [places, 2])
            self.var_eps = tiny(name + "_var_eps", [places])
            self.rstd = tiny(name + "_rstd", [places])
            self.stats_done = sem(name + "_stats_done")
            self.moments_done = sem(name + "_moments_done")
            self.eps_added = sem(name + "_eps_added")
            self.rstd_done = sem(name + "_rstd_done")

    norm_x = Norm("norm_x", TPB)
    norm_a = Norm("norm_a", 1)
    norm_t = Norm("norm_t", TPB)
    norm_y = Norm("norm_y", 1)

    ident_cleared, ident_ready, scalars_set = sem("ident_cleared"), sem("ident_ready"), sem("scalars_set")
    bqk_loaded, bv_loaded, bo_loaded = sem("bqk_loaded"), sem("bv_loaded"), sem("bo_loaded")
    wqkv_loaded = [sem("wqkv_loaded0"), sem("wqkv_loaded1")]
    wqkv_high, wqkv_low = sem("wqkv_high"), sem("wqkv_low")
    wo_loaded, wo_high, wo_low = sem("wo_loaded"), sem("wo_high"), sem("wo_low")
    x_loaded = [sem(f"x_loaded{i}") for i in range(TPB)]
    xn_done, xt_ready, xt_high, xt_low = sem("xn_done"), sem("xt_ready"), sem("xt_high"), sem("xt_low")
    qk_ready, q_copied, k_high, k_low = sem("qk_ready"), sem("q_copied"), sem("k_high"), sem("k_low")
    v_ready, v_halved, v_summed = sem("v_ready"), sem("v_halved"), sem("v_summed")
    v_high, v_low = sem("v_high"), sem("v_low")
    q_high, q_low, s_ready = sem("q_high"), sem("q_low"), sem("s_ready")
    bank_maxed, row_maxed, max_negated = sem("bank_maxed"), sem("row_maxed"), sem("max_negated")
    exp_done, sum_done, sum_inverted = sem("exp_done"), sem("sum_done"), sem("sum_inverted")
    pt_ready, pt_high, pt_low = sem("pt_ready"), sem("pt_high"), sem("pt_low")
    pv_ready, o_halved, o_ready = sem("pv_ready"), sem("o_halved"), sem("o_ready")
    ot_ready, ot_high, ot_low = sem("ot_ready"), sem("ot_high"), sem("ot_low")
    a_ready, a_copied, a_normed = sem("a_ready"), sem("a_copied"), sem("a_normed")
    x_res_loaded, x1_ready = sem("x_res_loaded"), sem("x1_ready")
    stored = sem("stored")
    w_loaded = [sem("w_loaded0"), sem("w_loaded1")]
    w_high, w_low, item_used = sem("w_high"), sem("w_low"), sem("item_used")
    t_loaded = [sem(f"t_loaded{i}") for i in range(TPB)]
    r_loaded = sem("r_loaded")
    x1n_done, x1t_ready = sem("x1n_done"), sem("x1t_ready")
    x1t_high, x1t_low = sem("x1t_high"), sem("x1t_low")
    gate_ready, silu_done, prod_done = sem("gate_ready"), sem("silu_done"), sem("prod_done")
    h_high, h_low, rest_split = sem("h_high"), sem("h_low"), sem("rest_split")
    y_ready, y_copied, y_normed, y_added = sem("y_ready"), sem("y_copied"), sem("y_normed"), sem("y_added")

    def cols(i, width=P):
        return bass.ds(i * width, width) if type(i) is not int else slice(i * width, (i + 1) * width)

    def three(pe, dst, stat, mov, first, last):
        pe.matmul(dst, stat(HIGH), mov(HIGH), start=first, stop=False)
        pe.matmul(dst, stat(HIGH), mov(LOW), start=False, stop=False)
        return pe.matmul(dst, stat(LOW), mov(HIGH), start=False, stop=last)

    SHORT = UPS + DOWN
    half_items = (0, SHORT, SHORT + 1)

    with nc.Block() as block:

        @block.sync
        def _(sp):
            def load_x(row, i):
                sp.dma_start(x_tile[:, i, :], x[bass.ds(row, P), :]).then_inc(x_loaded[i], 16)

            def load_wqkv(h):
                sp.dma_start(wqkv_raw[:, h, :, :], wqkv[h]).then_inc(wqkv_loaded[h], 16)

            load_x(0, 0)
            load_x(P, 1)
            load_wqkv(0)
            load_x(2 * P, 2)
            load_x(3 * P, 3)
            load_wqkv(1)
            sp.dma_start(bqk_sb[:], bqk[:, :]).then_inc(bqk_loaded, 16)
            sp.dma_start(bv_sb[:], bv[:, :]).then_inc(bv_loaded, 16)
            with sp.Fori(0, BLOCKS - 1) as b:
                for i in range(TPB):
                    sp.wait_ge(xt_ready, b * (2 * TPB) + (2 * i + 2))
                    load_x(b * BLOCK + (BLOCK + i * P), i)

            sp.wait_ge(k_low, KD * BLOCKS)
            sp.wait_ge(v_low, TILES)
            sp.dma_start(wo_raw[:], wo[:, :, :]).then_inc(wo_loaded, 16)
            sp.dma_start(bo_sb[:], bo[:, :]).then_inc(bo_loaded, 16)

            def load_item(s, slot):
                if type(s) is int and s in half_items:
                    sp.dma_start(w_raw[:, slot, 0:ITEM // 2], wffn[s, :, 0:ITEM // 2]).then_inc(w_loaded[slot], 16)
                else:
                    sp.dma_start(w_raw[:, slot, :], wffn[s, :, :]).then_inc(w_loaded[slot], 16)

            def load_residual(t):
                sp.dma_start(x_res[:], x[bass.ds(t * P, P), :]).then_inc(x_res_loaded, 16)

            def store_x1(t):
                sp.wait_ge(x1_ready, t + 1)
                sp.dma_start(x1_dram[bass.ds(t * P, P), :], x1_tile[:]).then_inc(stored, 16)

            def next_residual(t):
                sp.wait_ge(stored, t * 16 + 16)
                load_residual(t + 1)

            load_residual(0)
            load_item(0, 0)
            load_item(1, 1)
            with sp.Fori(0, TILES - TPB) as t:
                store_x1(t)
                next_residual(t)

            def load_t(b, i):
                sp.dma_start(t_tile[:, i, :], x1_dram[bass.ds(b * BLOCK + i * P, P), :]).then_inc(t_loaded[i], 16)

            def load_r(b, i):
                sp.dma_start(t_tile[:, i, :], x1_dram[bass.ds(b * BLOCK + i * P, P), :]).then_inc(r_loaded, 16)

            sp.wait_ge(q_low, TILES)
            for i in range(TPB):
                load_t(0, i)
            with sp.Fori(TILES - TPB, TILES - 1) as t:
                store_x1(t)
                next_residual(t)
            store_x1(TILES - 1)
            sp.wait_ge(stored, 16 * TILES)

            def tick(b, s, slot):
                sp.wait_ge(w_low, b * (2 * ITEMS) + s * 2 + 2)
                load_item((s + 2) % ITEMS if type(s) is int else s + 2, slot)

            def up(b, post):
                if post is not None:
                    sp.wait_ge(x1t_ready, b * (2 * TPB) + 2 * TPB)
                    for i in range(TPB):
                        load_r(post, i)
                tick(b, 0, 0)
                tick(b, 1, 1)
                if post is not None:
                    with sp.Fori(0, TPB) as i:
                        tick(b, i * 2 + 2, 0)
                        tick(b, i * 2 + 3, 1)
                        sp.wait_ge(y_added, post * TPB + i + 1)
                        sp.dma_start(out[bass.ds(post * BLOCK + i * P, P), :], y_tile[:, i, :]).then_inc(stored, 16)
                with sp.Fori(0 if post is None else TPB, FULL // 2) as p:
                    tick(b, p * 2 + 2, 0)
                    tick(b, p * 2 + 3, 1)

            def down(b, more):
                if more:
                    sp.wait_ge(x1t_ready, b * (2 * TPB) + 2 * TPB)
                    for i in range(TPB):
                        load_t(b + 1, i)
                else:
                    for i in range(TPB):
                        load_r(b, i)
                for s in range(UPS, ITEMS if more else ITEMS - 2):
                    tick(b, s, s % 2)

            up(0, None)
            with sp.Fori(0, BLOCKS - 1) as b:
                down(b, True)
                up(b + 1, b)
            down(BLOCKS - 1, False)
            with sp.Fori(0, TPB) as i:
                sp.wait_ge(y_added, i + ((BLOCKS - 1) * TPB + 1))
                sp.dma_start(out[bass.ds(i * P + (BLOCKS - 1) * BLOCK, P), :], y_tile[:, i, :]).then_inc(stored, 16)
            sp.wait_ge(stored, 16 * 2 * TILES)

        @block.gpsimd
        def _(pool):
            pool.memset(ident[:], 0.0).then_inc(ident_cleared, 1)
            pool.memset(minus_half[:], -0.5)
            pool.memset(eps[:], EPS).then_inc(scalars_set, 1)
            pool.wait_ge(ident_cleared, 1)
            pool.affine_select(out=ident[:], in_=ident[:], compare_op=ALU.not_equal, fill=1.0, base=0,
                               pattern=[[-1, P]], channel_multiplier=1).then_inc(ident_ready, 1)
            pool.wait_ge(scalars_set, 1)

            def rstd(norm, n, i):
                pool.wait_ge(norm.moments_done, n + 1)
                pool.tensor_tensor(norm.var_eps[:, i:i + 1], norm.moments[:, i, 1:2], eps[:],
                                   ALU.add).then_inc(norm.eps_added, 1)
                pool.wait_ge(norm.eps_added, n + 1)
                pool.tensor_tensor(norm.rstd[:, i:i + 1], norm.var_eps[:, i:i + 1], minus_half[:],
                                   ALU.pow).then_inc(norm.rstd_done, 1)

            def sum_x1(t):
                pool.wait_ge(x_res_loaded, t * 16 + 16)
                pool.wait_ge(a_normed, t + 1)
                pool.tensor_tensor(x1_tile[:], x1_tile[:], x_res[:], ALU.add).then_inc(x1_ready, 1)

            def sum_y(b, i):
                pool.wait_ge(r_loaded, b * (16 * TPB) + 16 * TPB)
                pool.wait_ge(y_normed, b * TPB + i + 1)
                pool.tensor_tensor(y_tile[:, i, :], y_tile[:, i, :], t_tile[:, i, :], ALU.add).then_inc(y_added, 1)

            with pool.Fori(0, BLOCKS) as b:
                for i in range(TPB):
                    rstd(norm_x, b * TPB + i, i)
            with pool.Fori(0, TILES - 2) as t:
                rstd(norm_a, t, 0)
                sum_x1(t)
            for t in (TILES - 2, TILES - 1):
                for i in (0, 1):
                    rstd(norm_t, 2 * (t - TILES + 2) + i, 2 * (t - TILES + 2) + i)
                rstd(norm_a, t, 0)
                sum_x1(t)

            def outputs(b):
                with pool.Fori(0, TPB) as i:
                    rstd(norm_y, b * TPB + i, 0)
                    sum_y(b, i)

            with pool.Fori(0, BLOCKS - 1) as b:
                for i in range(TPB):
                    rstd(norm_t, b * TPB + (TPB + i), i)
                outputs(b)
            outputs(BLOCKS - 1)

        @block.scalar
        def _(act):
            def split_wqkv(h):
                act.wait_ge(wqkv_loaded[h], 16)
                k = slice(h * KC // 2, (h + 1) * KC // 2)
                act.copy(wqk[:, HIGH, k, :], wqkv_raw[:, h, :, 0:2 * D])
                act.copy(wv[:, k, HIGH, :], wqkv_raw[:, h, :, 2 * D:3 * D]).then_inc(wqkv_high, 1)

            def xt_tile(n, i):
                for g in (0, 1):
                    act.wait_ge(xt_ready, n * 2 + (g + 1))
                    act.copy(xn_t[:, HIGH, 4 * g:4 * g + 4, cols(i)],
                             ps[:, 6 + g, :].rearrange("p (k t) -> p k t", k=4)).then_inc(xt_high, 1)

            def qk_out(b):
                for m in range(2 * KD):
                    act.wait_ge(qk_ready, b * (2 * KD) + (m + 1))
                    d = m % KD
                    if m < KD:
                        act.activation(q_t[:, d, cols(b, BLOCK)], ps[:, m, :], ACT.Identity,
                                       bias=bqk_sb[:, m:m + 1]).then_inc(q_copied, 1)
                    else:
                        act.activation(k_t[:, d, HIGH, cols(b, BLOCK)], ps[:, m, :], ACT.Identity,
                                       bias=bqk_sb[:, m:m + 1]).then_inc(k_high, 1)

            def v_out(n, i):
                act.wait_ge(v_summed, n + 1)
                act.copy(v[:, n, HIGH, :], v_sum[:, i % 2, :]).then_inc(v_high, 1)

            xt_tile(0, 0)
            xt_tile(1, 1)
            split_wqkv(0)
            xt_tile(2, 2)
            xt_tile(3, 3)
            split_wqkv(1)
            act.wait_ge(bqk_loaded, 16)
            with act.Fori(0, BLOCKS - 1) as b:
                qk_out(b)
                for i in range(TPB):
                    v_out(b * TPB + i, i)
                    xt_tile(b * TPB + (TPB + i), i)
            qk_out(BLOCKS - 1)
            for i in range(TPB):
                v_out((BLOCKS - 1) * TPB + i, i)

            def q_split(t):
                if type(t) is not int or t > 0:
                    act.wait_ge(s_ready, t * 4)
                else:
                    act.wait_ge(q_copied, KD * BLOCKS)
                act.copy(q_tile[:, HIGH, :, :], q_t[:, :, cols(t)]).then_inc(q_high, 1)

            def split_item_high(b, s, slot, pair=None):
                whole = not (type(s) is int and s in half_items)
                pair = s // 2 if pair is None else pair
                act.wait_ge(w_loaded[slot], b * (16 * ITEMS // 2) + pair * 16 + 16)
                n = ITEM // 2
                if whole:
                    for p in (0, 1):
                        act.copy(w_sb[:, slot, HIGH, p * n:(p + 1) * n], w_raw[:, slot, p * n:(p + 1) * n]).then_inc(w_high, 1)
                else:
                    act.copy(w_sb[:, slot, HIGH, 0:n], w_raw[:, slot, 0:n]).then_inc(w_high, 2)

            def attend(t):
                inner = type(t) is not int
                if inner or 2 <= t:
                    act.wait_ge(ot_ready, t - 1)
                    act.copy(o_t[:, HIGH, :, :], ps[:, 7, 0:D].rearrange("p (k t) -> p k t", k=KD)).then_inc(ot_high, 1)
                if inner or 1 <= t <= TILES:
                    for g in range(4):
                        act.wait_ge(pt_ready, t * 4 + (g - 3))
                        act.copy(probs_t[:, HIGH, 4 * g:4 * g + 4, :],
                                 ps[:, 4 + g % 2, :].rearrange("p (k t) -> p k t", k=4)).then_inc(pt_high, 1)
                if inner or t < TILES - 1:
                    q_split(t + 1)
                if inner or t < TILES:
                    act.wait_ge(max_negated, t + 1)
                    for g in range(4):
                        act.activation(probs[:, cols(g, BANK)], ps[:, g, :], ACT.Exp, bias=neg_max[:],
                                       scale=float(D) ** -0.5, accum_out=bank_sum[:, g:g + 1]).then_inc(exp_done, 1)
                if inner or 1 <= t <= TILES:
                    act.wait_ge(sum_inverted, t)
                    act.wait_ge(pv_ready, t)
                    act.activation(o_half[:], ps[:, 6, D:2 * D], ACT.Copy, scale=inv_sum[:]).then_inc(o_halved, 1)

            q_split(0)
            attend(0)
            attend(1)
            act.wait_ge(wo_loaded, 16)
            act.copy(wo_sb[:, HIGH, :, :], wo_raw[:]).then_inc(wo_high, 1)
            split_item_high(0, 0, 0)
            with act.Fori(2, TILES - 1) as t:
                attend(t)
            attend(TILES - 1)
            attend(TILES)

            def x1t_tile(n, i):
                for g in (0, 1):
                    act.wait_ge(x1t_ready, n * 2 + (g + 1))
                    act.copy(x1n_t[:, HIGH, 4 * g:4 * g + 4, cols(i)],
                             ps[:, 2 * (i % 2) + g, :].rearrange("p (k t) -> p k t", k=4)).then_inc(x1t_high, 1)

            for i in range(TPB):
                x1t_tile(i, i)
            attend(TILES + 1)

            def tick(b, s, slot, pair=None):
                if not (type(b) is int and type(s) is int and b == 0 and s == 0):
                    act.wait_ge(item_used, b * ITEMS + s)
                if type(s) is int and s == ITEMS - 1:
                    split_item_high(b + 1, 0, 0)
                else:
                    split_item_high(b, s + 1, 1 - slot, pair)

            def silu(b, c, slot):
                act.wait_ge(gate_ready, b * FULL + c + 1)
                if type(c) is not int or c > 0:
                    act.wait_ge(prod_done, b * UPS + c)
                act.activation(silu_sb[:, slot, :], ps[:, 2 * slot, :], ACT.Silu).then_inc(silu_done, 1)

            def silu_rest(b):
                act.wait_ge(item_used, b * ITEMS + 1)
                act.activation(silu_sb[REST:P, 0, :], ps[0:REST, 0, :], ACT.Silu).then_inc(silu_done, 1)

            def up(b):
                tick(b, 0, 0)
                tick(b, 1, 1)
                silu_rest(b)
                with act.Fori(0, FULL // 2) as p:
                    tick(b, p * 2 + 2, 0, p + 1)
                    silu(b, p * 2, 1)
                    tick(b, p * 2 + 3, 1, p + 2)
                    silu(b, p * 2 + 1, 0)

            def y_out(i, half, bank):
                act.copy(y_tile[:, i, cols(half, BANK)], ps[:, bank, :]).then_inc(y_copied, 1)

            def down(b, more):
                for s in range(UPS, ITEMS):
                    if s < ITEMS - 1 or more:
                        tick(b, s, s % 2)
                    if s == UPS:
                        silu(b, FULL - 1, 1)
                    if more and UPS < s <= UPS + TPB:
                        x1t_tile(b * TPB + (s - UPS - 1 + TPB), s - UPS - 1)
                    if s == SHORT + 1:
                        act.wait_ge(stored, b * (16 * TPB) + 16 * TILES)
                        for i in range(TPB):
                            y_out(i, 0, TPB + i)
                for i in range(TPB):
                    if i < TPB - 1:
                        act.wait_ge(y_ready, b * (TPB - 1) + (i + 1))
                    else:
                        act.wait_ge(item_used, b * ITEMS + ITEMS)
                    y_out(i, 1, i)

            up(0)
            with act.Fori(0, BLOCKS - 1) as b:
                down(b, True)
                up(b + 1)
            down(BLOCKS - 1, False)

        @block.vector
        def _(dve):
            def row_stats(norm, i, src):
                for h in range(HALF):
                    dve.bn_stats(norm.stats[:, i, h, :], src[:, cols(h, BANK)]).then_inc(norm.stats_done, 1)

            def stats_in(norm, n):
                dve.wait_ge(norm.stats_done, n * 2 + 2)

            def moments(norm, i):
                dve.bn_aggr(norm.moments[:, i, :], norm.stats[:, i, :, :]).then_inc(norm.moments_done, 1)

            def normed(norm, n, i, src, done):
                dve.wait_ge(norm.rstd_done, n + 1)
                dve.tensor_scalar(src, src, norm.moments[:, i, 0:1], norm.rstd[:, i:i + 1],
                                  ALU.subtract, ALU.mult).then_inc(done, 1)

            def low(dst, src, high):
                return dve.tensor_tensor(dst, src, high.bitcast(F32), ALU.subtract)

            def x_stats(i, round_):
                dve.wait_ge(x_loaded[i], round_ * 16 + 16)
                row_stats(norm_x, i, x_tile[:, i, :])

            def x_normed(n, i):
                normed(norm_x, n, i, x_tile[:, i, :], xn_done)

            def split_wqkv(h):
                dve.wait_ge(wqkv_high, h + 1)
                k = slice(h * KC // 2, (h + 1) * KC // 2)
                low(wqk[:, LOW, k, :], wqkv_raw[:, h, :, 0:2 * D], wqk[:, HIGH, k, :])
                low(wv[:, k, LOW, :], wqkv_raw[:, h, :, 2 * D:3 * D], wv[:, k, HIGH, :]).then_inc(wqkv_low, 1)

            def xt_tile(n, i):
                for g in (0, 1):
                    dve.wait_ge(xt_high, n * 2 + (g + 1))
                    k = slice(4 * g, 4 * g + 4)
                    low(xn_t[:, LOW, k, cols(i)], ps[:, 6 + g, :].rearrange("p (k t) -> p k t", k=4),
                        xn_t[:, HIGH, k, cols(i)]).then_inc(xt_low, 1)

            def k_split(b):
                for d in range(KD):
                    dve.wait_ge(k_high, b * KD + (d + 1))
                    m = KD + d
                    dve.scalar_tensor_tensor(out=k_t[:, d, LOW, cols(b, BLOCK)], in0=ps[:, m, :],
                                             scalar=bqk_sb[:, m:m + 1],
                                             in1=k_t[:, d, HIGH, cols(b, BLOCK)].bitcast(F32),
                                             op0=ALU.add, op1=ALU.subtract).then_inc(k_low, 1)

            def v_add(n, i):
                dve.wait_ge(v_ready, n + 1)
                bank = ps[:, 4 + i % 2, :]
                dve.tensor_tensor(v_half[:], bank[:, D:2 * D], bv_sb[:], ALU.add).then_inc(v_halved, 1)
                dve.wait_ge(v_halved, n + 1)
                dve.tensor_tensor(v_sum[:, i % 2, :], bank[:, 0:D], v_half[:], ALU.add).then_inc(v_summed, 1)

            def v_split(n, i):
                dve.wait_ge(v_high, n + 1)
                low(v[:, n, LOW, :], v_sum[:, i % 2, :], v[:, n, HIGH, :]).then_inc(v_low, 1)

            def norm_block(b):
                x_stats(0, b)
                for i in range(1, TPB):
                    stats_in(norm_x, b * TPB + (i - 1))
                    x_stats(i, b)
                    moments(norm_x, i - 1)
                stats_in(norm_x, b * TPB + (TPB - 1))
                x_normed(b * TPB, 0)
                moments(norm_x, TPB - 1)
                for i in range(1, TPB):
                    x_normed(b * TPB + i, i)

            norm_block(0)
            xt_tile(0, 0)
            xt_tile(1, 1)
            split_wqkv(0)
            xt_tile(2, 2)
            xt_tile(3, 3)
            split_wqkv(1)
            dve.wait_ge(bqk_loaded, 16)
            dve.wait_ge(bv_loaded, 16)
            with dve.Fori(0, BLOCKS - 1) as b:
                norm_block(b + 1)
                k_split(b)
                for i in range(TPB):
                    v_add(b * TPB + i, i)
                    xt_tile(b * TPB + (TPB + i), i)
                    v_split(b * TPB + i, i)
            k_split(BLOCKS - 1)
            for i in range(TPB):
                n = (BLOCKS - 1) * TPB + i
                v_add(n, i)
                v_split(n, i)

            def q_split(t):
                dve.wait_ge(q_high, t + 1)
                low(q_tile[:, LOW, :, :], q_t[:, :, cols(t)], q_tile[:, HIGH, :, :]).then_inc(q_low, 1)

            def split_item_low(b, s, slot):
                whole = not (type(s) is int and s in half_items)
                n = ITEM // 2
                for p in ((0, 1) if whole else (0,)):
                    dve.wait_ge(w_high, b * (2 * ITEMS) + s * 2 + (p + 1))
                    part = slice(p * n, (p + 1) * n)
                    low(w_sb[:, slot, LOW, part], w_raw[:, slot, part],
                        w_sb[:, slot, HIGH, part]).then_inc(w_low, 1 if whole else 2)

            def attend(t):
                inner = type(t) is not int
                now, before, older = (inner or t < TILES), (inner or 1 <= t <= TILES), (inner or 2 <= t)
                if before:
                    dve.wait_ge(exp_done, t * 4)
                    dve.reduce_sum(row_sum[:], bank_sum[:], AX.X).then_inc(sum_done, 1)
                    dve.wait_ge(sum_done, t)
                    dve.reciprocal(inv_sum[:], row_sum[:]).then_inc(sum_inverted, 1)
                if older:
                    dve.wait_ge(ot_high, t - 1)
                    low(o_t[:, LOW, :, :], ps[:, 7, 0:D].rearrange("p (k t) -> p k t", k=KD),
                        o_t[:, HIGH, :, :]).then_inc(ot_low, 1)
                for g in range(4):
                    if now:
                        dve.wait_ge(s_ready, t * 4 + (g + 1))
                        dve.reduce_max(bank_max[:, g:g + 1], ps[:, g, :], AX.X).then_inc(bank_maxed, 1)
                    if now and g == 3:
                        dve.wait_ge(bank_maxed, t * 4 + 4)
                        dve.reduce_max(row_max[:], bank_max[:], AX.X).then_inc(row_maxed, 1)
                        dve.wait_ge(row_maxed, t + 1)
                        dve.tensor_scalar(neg_max[:], row_max[:], -float(D) ** -0.5, None,
                                          ALU.mult).then_inc(max_negated, 1)
                    if before:
                        dve.wait_ge(pt_high, t * 4 + (g - 3))
                        k = slice(4 * g, 4 * g + 4)
                        low(probs_t[:, LOW, k, :], ps[:, 4 + g % 2, :].rearrange("p (k t) -> p k t", k=4),
                            probs_t[:, HIGH, k, :]).then_inc(pt_low, 1)
                if not inner and t < TILES - 1:
                    q_split(t + 1)
                if older:
                    dve.wait_ge(x_res_loaded, t * 16 - 16)
                    for h in range(HALF):
                        dve.wait_ge(a_ready, t * 2 + (h - 3))
                        dve.tensor_tensor(x1_tile[:, cols(h, BANK)], ps[:, 4 + h, :], bo_sb[:, cols(h, BANK)],
                                          ALU.add).then_inc(a_copied, 1)
                    dve.wait_ge(a_copied, t * 2 - 2)
                    row_stats(norm_a, 0, x1_tile)
                    stats_in(norm_a, t - 2)
                    if inner:
                        q_split(t + 1)
                    moments(norm_a, 0)
                if before:
                    dve.wait_ge(o_halved, t)
                    dve.scalar_tensor_tensor(out=o_sum[:], in0=ps[:, 6, 0:D], scalar=inv_sum[:], in1=o_half[:],
                                             op0=ALU.mult, op1=ALU.add).then_inc(o_ready, 1)
                if older:
                    normed(norm_a, t - 2, 0, x1_tile[:], a_normed)

            q_split(0)
            attend(0)
            attend(1)
            dve.wait_ge(wo_high, 1)
            low(wo_sb[:, LOW, :, :], wo_raw[:], wo_sb[:, HIGH, :, :]).then_inc(wo_low, 1)
            split_item_low(0, 0, 0)
            dve.wait_ge(bo_loaded, 16)
            with dve.Fori(2, TILES - 1) as t:
                attend(t)
            attend(TILES - 1)

            def t_stats(b, i):
                dve.wait_ge(t_loaded[i], b * 16 + 16)
                row_stats(norm_t, i, t_tile[:, i, :])

            def t_stats_in(b, i):
                stats_in(norm_t, b * TPB + i)

            def t_normed(b, i):
                normed(norm_t, b * TPB + i, i, t_tile[:, i, :], x1n_done)

            def t_pair(b, i):
                t_stats(b, i)
                t_stats_in(b, i)
                t_stats(b, i + 1)
                moments(norm_t, i)
                t_normed(b, i)

            def t_second(b, i):
                moments(norm_t, i)
                t_normed(b, i)

            t_pair(0, 0)
            t_stats_in(0, 1)
            t_second(0, 1)
            attend(TILES)
            t_pair(0, 2)
            t_stats_in(0, 3)
            t_second(0, 3)

            def x1t_tile(n, i):
                for g in (0, 1):
                    dve.wait_ge(x1t_high, n * 2 + (g + 1))
                    k = slice(4 * g, 4 * g + 4)
                    low(x1n_t[:, LOW, k, cols(i)], ps[:, 2 * (i % 2) + g, :].rearrange("p (k t) -> p k t", k=4),
                        x1n_t[:, HIGH, k, cols(i)]).then_inc(x1t_low, 1)

            for i in range(TPB):
                x1t_tile(i, i)
            attend(TILES + 1)

            def tick(b, s, slot):
                if type(s) is int and s == ITEMS - 1:
                    split_item_low(b + 1, 0, 0)
                else:
                    split_item_low(b, s + 1, 1 - slot)

            def hidden(b, c, slot):
                dve.wait_ge(h_low, b * UPS + c + 1)
                dve.wait_ge(silu_done, b * UPS + c + 2)
                dve.wait_ge(item_used, b * ITEMS + c + 2)
                dve.tensor_tensor(h_f32[:], silu_sb[:, slot, :], ps[:, 2 * slot + 1, :], ALU.mult).then_inc(prod_done, 1)
                dve.wait_ge(prod_done, b * UPS + c + 2)
                dve.tensor_copy(h_t[:, c, HIGH, :], h_f32[:]).then_inc(h_high, 1)
                dve.wait_ge(h_high, b * UPS + c + 2)
                low(h_t[:, c, LOW, :], h_f32[:], h_t[:, c, HIGH, :]).then_inc(h_low, 1)

            def hidden_rest(b):
                up_half = slice(REST, P)
                dve.wait_ge(silu_done, b * UPS + 1)
                dve.tensor_tensor(h_f32[up_half, :], silu_sb[up_half, 0, :], ps[up_half, 0, :],
                                  ALU.mult).then_inc(prod_done, 1)
                dve.wait_ge(prod_done, b * UPS + 1)
                dve.tensor_copy(h_rest[0:REST, :], h_f32[up_half, :])
                dve.tensor_copy(h_rest[up_half, :], h_f32[up_half, :]).then_inc(h_high, 1)
                dve.wait_ge(h_high, b * UPS + 1)
                low(h_rest[up_half, :], h_f32[up_half, :], h_rest[up_half, :]).then_inc(h_low, 1)

            def y_stats(b, i):
                dve.wait_ge(y_copied, b * (2 * TPB) + i + (TPB + 1))
                row_stats(norm_y, 0, y_tile[:, i, :])

            def y_norm(b, i):
                normed(norm_y, b * TPB + i, 0, y_tile[:, i, :], y_normed)

            def up(b, post):
                tick(b, 0, 0)
                tick(b, 1, 1)
                hidden_rest(b)
                if post is not None:
                    with dve.Fori(0, TPB) as i:
                        tick(b, i * 2 + 2, 0)
                        hidden(b, i * 2, 1)
                        y_stats(post, i)
                        stats_in(norm_y, post * TPB + i)
                        tick(b, i * 2 + 3, 1)
                        moments(norm_y, 0)
                        hidden(b, i * 2 + 1, 0)
                        y_norm(post, i)
                with dve.Fori(0 if post is None else TPB, FULL // 2) as p:
                    tick(b, p * 2 + 2, 0)
                    hidden(b, p * 2, 1)
                    tick(b, p * 2 + 3, 1)
                    hidden(b, p * 2 + 1, 0)

            def down(b, more):
                for s in range(UPS, ITEMS):
                    if more and s in (UPS + 1, UPS + 3):
                        t_stats_in(b + 1, s - UPS)
                    if s < ITEMS - 1 or more:
                        tick(b, s, s % 2)
                    if s == UPS:
                        hidden(b, FULL - 1, 1)
                    if more and s in (UPS, UPS + 2):
                        t_pair(b + 1, s - UPS)
                    if more and s in (UPS + 1, UPS + 3):
                        t_second(b + 1, s - UPS)
                    if more and UPS < s <= UPS + TPB:
                        x1t_tile(b * TPB + (s - UPS - 1 + TPB), s - UPS - 1)

            up(0, None)
            with dve.Fori(0, BLOCKS - 1) as b:
                down(b, True)
                up(b + 1, b)
            down(BLOCKS - 1, False)
            for i in range(TPB):
                y_stats(BLOCKS - 1, i)
                stats_in(norm_y, (BLOCKS - 1) * TPB + i)
                moments(norm_y, 0)
                y_norm(BLOCKS - 1, i)

        @block.tensor
        def _(pe):
            pe.wait_ge(ident_ready, 1)

            def transposes(bank, k0, src, count):
                for j in range(count):
                    last = pe.transpose(ps[:, bank, cols(j)], src[:, cols(k0 + j)], ident[:])
                return last

            def xt_tile(n, i):
                pe.wait_ge(xn_done, n + 1)
                for g in (0, 1):
                    if i > 0:
                        pe.wait_ge(xt_low, n * 2 + (g - 1))
                    transposes(6 + g, 4 * g, x_tile[:, i, :], 4).then_inc(xt_ready, 1)

            def qk(b):
                pe.wait_ge(xt_low, b * (2 * TPB) + 2 * TPB)
                for m in range(2 * KD):
                    for k in range(KC):
                        last = three(pe, ps[:, m, :], lambda p: wqk[:, p, k, cols(m)], lambda p: xn_t[:, p, k, :],
                                     k == 0, k == KC - 1)
                    last.then_inc(qk_ready, 1)

            def project_v(n, i):
                bank = ps[:, 4 + i % 2, :]
                if i > 1:
                    pe.wait_ge(v_summed, n - 1)
                for k in range(KC):
                    pe.matmul(bank, xn_t[:, HIGH, k, cols(i)], wv[:, k, :, :], start=k == 0, stop=False)
                    last = pe.matmul(bank[:, 0:D], xn_t[:, LOW, k, cols(i)], wv[:, k, HIGH, :],
                                     start=False, stop=k == KC - 1)
                last.then_inc(v_ready, 1)

            for i in range(TPB):
                xt_tile(i, i)
            pe.wait_ge(wqkv_low, 2)
            with pe.Fori(0, BLOCKS - 1) as b:
                qk(b)
                for i in range(TPB):
                    project_v(b * TPB + i, i)
                    xt_tile(b * TPB + (TPB + i), i)
            qk(BLOCKS - 1)
            for i in range(TPB):
                project_v((BLOCKS - 1) * TPB + i, i)

            def attend(t):
                inner = type(t) is not int
                now, before, older = (inner or t < TILES), (inner or 1 <= t <= TILES), (inner or 2 <= t)
                if now:
                    pe.wait_ge(q_low, t + 1)
                for g in range(4):
                    if before:
                        pe.wait_ge(exp_done, t * 4 + (g - 3))
                    if now:
                        for d in range(KD):
                            last = three(pe, ps[:, g, :], lambda p: q_tile[:, p, d, :],
                                         lambda p: k_t[:, d, p, cols(g, BANK)], d == 0, d == KD - 1)
                        last.then_inc(s_ready, 1)
                    if older and g == 0:
                        pe.wait_ge(o_ready, t - 1)
                        transposes(7, 0, o_sum, KD).then_inc(ot_ready, 1)
                    if before:
                        if g > 1:
                            pe.wait_ge(pt_low, t * 4 + (g - 5))
                        transposes(4 + g % 2, 4 * g, probs, 4).then_inc(pt_ready, 1)
                if older:
                    pe.wait_ge(ot_low, t - 1)
                    for h in range(HALF):
                        if before:
                            pe.wait_ge(pt_low, t * 4 + (h - 1))
                        for d in range(KD):
                            last = three(pe, ps[:, 4 + h, :], lambda p: o_t[:, p, d, :],
                                         lambda p: wo_sb[:, p, d, cols(h, BANK)], d == 0, d == KD - 1)
                        last.then_inc(a_ready, 1)
                if before:
                    pe.wait_ge(pt_low, t * 4)
                    for k in range(TILES):
                        pe.matmul(ps[:, 6, :], probs_t[:, HIGH, k, :], v[:, k, :, :], start=k == 0, stop=False)
                        last = pe.matmul(ps[:, 6, 0:D], probs_t[:, LOW, k, :], v[:, k, HIGH, :],
                                         start=False, stop=k == TILES - 1)
                    last.then_inc(pv_ready, 1)

            pe.wait_ge(k_low, KD * BLOCKS)
            attend(0)
            pe.wait_ge(v_low, TILES)
            attend(1)
            pe.wait_ge(wo_low, 1)
            with pe.Fori(2, TILES) as t:
                attend(t)
            attend(TILES)

            def x1t_tile(n, i, fresh):
                pe.wait_ge(x1n_done, n + 1)
                for g in (0, 1):
                    if i > 1:
                        pe.wait_ge(x1t_low, n * 2 + (g - 3))
                    transposes(2 * (i % 2) + g, 4 * g, t_tile[:, i, :], 4).then_inc(x1t_ready, 1)

            for i in range(TPB):
                x1t_tile(i, i, True)
            attend(TILES + 1)

            def up(b, post):
                pe.wait_ge(x1t_low, b * (2 * TPB) + 2 * TPB)
                if post is not None:
                    pe.wait_ge(y_copied, post * (2 * TPB) + (TPB + 1))
                pe.wait_ge(w_low, b * (2 * ITEMS) + 2)
                for k in range(KC):
                    last = three(pe, ps[:, 0, :], lambda p: w_sb[:, 0, p, cols(k)], lambda p: x1n_t[:, p, k, :],
                                 k == 0, k == KC - 1)
                last.then_inc(item_used, 1)

                def gate_up(c, slot, older):
                    if older:
                        pe.wait_ge(prod_done, b * UPS + c)
                    for part in (0, 1):
                        pe.wait_ge(w_low, b * (2 * ITEMS) + c * 2 + (part + 3))
                        for k in range(KC):
                            last = three(pe, ps[:, 2 * slot + part, :],
                                         lambda p: w_sb[:, slot, p, cols(part * KC + k)],
                                         lambda p: x1n_t[:, p, k, :], k == 0, k == KC - 1)
                        last.then_inc(item_used if part else gate_ready, 1)

                if post is not None:
                    pe.wait_ge(y_copied, post * (2 * TPB) + 2 * TPB)
                gate_up(0, 1, False)
                with pe.Fori(0, FULL // 2) as p:
                    gate_up(p * 2 + 1, 0, True)
                    gate_up(p * 2 + 2, 1, True)

            def down(b, more):
                def add_chunk(bank, i, c, w, first):
                    return three(pe, ps[:, bank, :], lambda p: h_t[:, c, p, cols(i)], w, first, False)

                def full_item(s, j, bank0, first, last):
                    slot = s % 2
                    pe.wait_ge(w_low, b * (2 * ITEMS) + (2 * s + 2))
                    for i in range(TPB):
                        for q in range(CPI):
                            c = CPI * j + q
                            mm = three(pe, ps[:, bank0 + i, :], lambda p: h_t[:, c, p, cols(i)],
                                       lambda p: w_sb[:, slot, p, cols(q, BANK)],
                                       first and q == 0, last and q == CPI - 1)
                        if last and i < TPB - 1:
                            mm.then_inc(y_ready, 1)
                    mm.then_inc(item_used, 1)

                def short_item(s, bank0, first, last):
                    slot = s % 2
                    pe.wait_ge(w_low, b * (2 * ITEMS) + (2 * s + 2))
                    for i in range(TPB):
                        three(pe, ps[:, bank0 + i, :], lambda p: h_t[:, FULL - 1, p, cols(i)],
                              lambda p: w_sb[:, slot, p, cols(0, BANK)], first, False)
                        for p in (HIGH, LOW):
                            mm = pe.matmul(ps[:, bank0 + i, :], h_rest[:, cols(i)], w_sb[:, slot, p, cols(1, BANK)],
                                           start=False, stop=last and p == LOW)
                    mm.then_inc(item_used, 1)

                for j in range(DOWN):
                    if more and j > 0:
                        if j == 1:
                            pe.wait_ge(prod_done, b * UPS + UPS)
                        x1t_tile(b * TPB + (TPB + j - 1), j - 1, False)
                    pe.wait_ge(h_low, b * UPS + (CPI * (j + 1) + 1))
                    full_item(UPS + j, j, TPB, j == 0, False)
                pe.wait_ge(h_low, b * UPS + UPS)
                short_item(SHORT, TPB, False, True)
                if more:
                    pe.wait_ge(x1t_low, b * (2 * TPB) + 4 * TPB)
                short_item(SHORT + 1, 0, True, False)
                for j in range(DOWN):
                    full_item(SHORT + 2 + j, j, 0, False, j == DOWN - 1)

            up(0, None)
            with pe.Fori(0, BLOCKS - 1) as b:
                down(b, True)
                up(b + 1, b)
            down(BLOCKS - 1, False)


def kernel(**inputs):
    import numpy as np
    import concourse.bacc as bacc
    from concourse.bass_utils import run_bass_kernel_spmd

    def chunks(a):
        return a.reshape(a.shape[0] // P, P, a.shape[1]).transpose(1, 0, 2)

    a = {name: np.asarray(value) for name, value in inputs.items()}
    wqkv = chunks(a["L0_attn_Wqkv"])
    bqkv = a["L0_attn_bqkv"]
    gate, up, down = a["L0_ffn_W_gate"].T, a["L0_ffn_W_up"].T, a["L0_ffn_W_down"].T
    short = UPS + DOWN
    wffn = np.zeros((ITEMS, P, ITEM), a["L0_ffn_W_gate"].dtype)
    wffn[0, :, 0:KC * P] = chunks(np.concatenate([gate[:, FULL * P:], up[:, FULL * P:]], 1)).reshape(P, -1)
    for c in range(FULL):
        f = slice(c * P, (c + 1) * P)
        wffn[1 + c, :, 0:KC * P] = chunks(gate[:, f]).reshape(P, -1)
        wffn[1 + c, :, KC * P:] = chunks(up[:, f]).reshape(P, -1)
    for h in range(HALF):
        part = down[:, h * BANK:(h + 1) * BANK]
        first = short + 2 if h else UPS
        for j in range(DOWN):
            wffn[first + j] = chunks(part[j * CPI * P:(j + 1) * CPI * P]).reshape(P, -1)
        wffn[short + h, :, 0:BANK] = part[(FULL - 1) * P:FULL * P]
        wffn[short + h, 0:REST, BANK:2 * BANK] = part[FULL * P:]
        wffn[short + h, REST:P, BANK:2 * BANK] = part[FULL * P:]

    arrays = {
        "x": a["L0_attn_x"].reshape(S, C),
        "wqkv": np.stack([wqkv[:, :KC // 2], wqkv[:, KC // 2:]]),
        "bqk": bqkv[0:2 * D].reshape(2 * KD, P).T,
        "bv": np.broadcast_to(bqkv[2 * D:], (P, D)),
        "wo": chunks(a["L0_attn_Wo"]),
        "bo": np.broadcast_to(a["L0_attn_bo"], (P, C)),
        "wffn": wffn,
    }
    arrays = {name: np.ascontiguousarray(value) for name, value in arrays.items()}
    nc = bacc.Bacc("TRN2", target_bir_lowering=False, num_devices=1)
    args = [nc.dram_tensor(name, value.shape, mybir.dt.from_np(value.dtype), kind="ExternalInput").ap()
            for name, value in arrays.items()]
    args.append(nc.dram_tensor("out", (S, C), F32, kind="ExternalOutput").ap())
    transformer_block(nc, *args)
    result = run_bass_kernel_spmd(nc, [arrays], core_ids=[0])
    return result.results[0]["out"].reshape(a["L0_attn_x"].shape)
```

```python
import concourse.bass as bass
from concourse import mybir

F32 = mybir.dt.float32
F32R = mybir.dt.float32r
ACT = mybir.ActivationFunctionType
ALU = mybir.AluOpType
AX = mybir.AxisListType

P = 128
S = 2048
C = 1024
D = 256
F = 2752
EPS = 1e-5
BANK = 512
KC = C // P
KD = D // P
WT = 3 * KD
TILES = S // P
BLOCK = 512
TPB = BLOCK // P
BLOCKS = S // BLOCK
FULL = F // P
REST = F - FULL * P
HALF = C // BANK
ITEM = 2048
CPI = ITEM // BANK
DOWN = (FULL - 1) // CPI
UPS = FULL + 1
ITEMS = UPS + HALF * (DOWN + 1)
HIGH, LOW = 0, 1
assert 2 * REST == P and FULL == CPI * DOWN + 1 and ITEMS % 2 == 0


def transformer_block(nc, x, wqkv, bqk, bv, wo, bo, wffn, out):
    KB = 1024
    base = -(-nc.sbuf_base // 64) * 64

    def at(name, kb, shape, dt=F32):
        return nc.alloc_sbuf_tensor_at(name, [P] + shape, dt, offset=base + int(kb * KB))

    q_t = at("q_t", 0, [KD, S])
    k_t = at("k_t", 16, [KD, 2, S], F32R)
    v = at("v", 48, [TILES, 2, D], F32R)
    xn_t = at("xn_t", 80, [2, KC, BLOCK], F32R)
    wqkv_raw = at("wqkv_raw", 112, [WT, KC, P])
    x_tile = at("x_tile", 136, [TPB, C])
    v_half = at("v_half", 152, [D])
    v_sum = at("v_sum", 153, [2, D])
    bv_sb = at("bv_sb", 155, [D])
    wqk = at("wqk", 156, [2, KC, 2 * D], F32R)
    wv = at("wv", 188, [KC, 2, D], F32R)
    probs_t = at("probs_t", 80, [2, TILES, P], F32R)
    x1_tile = at("x1_tile", 96, [C])
    x_res = at("x_res", 100, [C])
    bo_sb = at("bo_sb", 104, [C])
    wo_sb = at("wo_sb", 112, [2, KD, C], F32R)
    wo_raw = at("wo_raw", 128, [KD, C])
    probs = at("probs", 136, [S])
    q_tile = at("q_tile", 144, [2, KD, P], F32R)
    o_half = at("o_half", 146, [D])
    o_sum = at("o_sum", 147, [D])
    o_t = at("o_t", 108, [2, KD, P], F32R)
    t_tile = at("t_tile", 0, [TPB, C])
    x1n_t = at("x1n_t", 16, [2, KC, BLOCK], F32R)
    y_tile = at("y_tile", 48, [TPB, C])
    h_t = at("h_t", 64, [FULL, 2, BLOCK], F32R)
    h_rest = at("h_rest", 64 + 4 * FULL, [BLOCK], F32R)
    silu_sb = at("silu_sb", 150, [2, BLOCK])
    h_f32 = at("h_f32", 154, [BLOCK])
    w_raw = at("w_raw", 156, [2, ITEM])
    w_sb = at("w_sb", 172, [2, 2, ITEM], F32R)
    ident = at("ident", 204, [P])
    small = [204.5]

    def tiny(name, shape):
        size = 4
        for n in shape:
            size *= n
        t = at(name, small[0], shape)
        small[0] += -(-size // 32) * 32 / KB
        return t

    bqk_sb = tiny("bqk_sb", [2 * KD])
    minus_half = tiny("minus_half", [1])
    eps = tiny("eps", [1])
    bank_max = tiny("bank_max", [4])
    row_max = tiny("row_max", [1])
    neg_max = tiny("neg_max", [1])
    bank_sum = tiny("bank_sum", [4])
    row_sum = tiny("row_sum", [1])
    inv_sum = tiny("inv_sum", [1])

    ps = nc.alloc_psum_tensor("ps", [P, 8, BANK], F32)
    x1_dram = nc.dram_tensor("x1_dram", [S, C], F32)

    sem = nc.alloc_semaphore

    class Norm:

        def __init__(self, name, places):
            self.places = places
            self.stats = tiny(name + "_stats", [places, 2, 6])
            self.moments = tiny(name + "_moments", [places, 2])
            self.var_eps = tiny(name + "_var_eps", [places])
            self.rstd = tiny(name + "_rstd", [places])
            self.stats_done = sem(name + "_stats_done")
            self.moments_done = sem(name + "_moments_done")
            self.eps_added = sem(name + "_eps_added")
            self.rstd_done = sem(name + "_rstd_done")

    norm_x = Norm("norm_x", TPB)
    norm_a = Norm("norm_a", 1)
    norm_t = Norm("norm_t", TPB)
    norm_y = Norm("norm_y", TPB)

    ident_cleared, ident_ready, scalars_set = sem("ident_cleared"), sem("ident_ready"), sem("scalars_set")
    bqk_loaded, bv_loaded, bo_loaded = sem("bqk_loaded"), sem("bv_loaded"), sem("bo_loaded")
    wqkv_loaded = [sem(f"wqkv_loaded{m}") for m in range(WT)]
    wqkv_high, wqkv_low = sem("wqkv_high"), sem("wqkv_low")
    wo_loaded, wo_high, wo_low = sem("wo_loaded"), sem("wo_high"), sem("wo_low")
    x_loaded = [sem(f"x_loaded{i}") for i in range(TPB)]
    xn_done, xt_ready, xt_high, xt_low = sem("xn_done"), sem("xt_ready"), sem("xt_high"), sem("xt_low")
    qk_ready, q_copied, k_high, k_low = sem("qk_ready"), sem("q_copied"), sem("k_high"), sem("k_low")
    v_ready, v_halved, v_summed = sem("v_ready"), sem("v_halved"), sem("v_summed")
    v_high, v_low = sem("v_high"), sem("v_low")
    q_high, q_low, s_ready = sem("q_high"), sem("q_low"), sem("s_ready")
    bank_maxed, row_maxed, max_negated = sem("bank_maxed"), sem("row_maxed"), sem("max_negated")
    exp_done, sum_done, sum_inverted = sem("exp_done"), sem("sum_done"), sem("sum_inverted")
    pt_ready, pt_high, pt_low = sem("pt_ready"), sem("pt_high"), sem("pt_low")
    pv_ready, o_halved, o_ready = sem("pv_ready"), sem("o_halved"), sem("o_ready")
    ot_ready, ot_high, ot_low = sem("ot_ready"), sem("ot_high"), sem("ot_low")
    a_ready, a_copied, a_normed = sem("a_ready"), sem("a_copied"), sem("a_normed")
    x_res_loaded, x1_ready = sem("x_res_loaded"), sem("x1_ready")
    stored = sem("stored")
    w_loaded = [sem("w_loaded0"), sem("w_loaded1")]
    w_high, w_low, item_used = sem("w_high"), sem("w_low"), sem("item_used")
    t_loaded = [sem(f"t_loaded{i}") for i in range(TPB)]
    r_loaded = sem("r_loaded")
    x1n_done, x1t_ready = sem("x1n_done"), sem("x1t_ready")
    x1t_high, x1t_low = sem("x1t_high"), sem("x1t_low")
    gate_ready, silu_done, prod_done = sem("gate_ready"), sem("silu_done"), sem("prod_done")
    h_high, h_low, rest_split = sem("h_high"), sem("h_low"), sem("rest_split")
    y_ready, y_copied, y_normed, y_added = sem("y_ready"), sem("y_copied"), sem("y_normed"), sem("y_added")

    def cols(i, width=P):
        return bass.ds(i * width, width) if type(i) is not int else slice(i * width, (i + 1) * width)

    def three(pe, dst, stat, mov, first, last):
        pe.matmul(dst, stat(HIGH), mov(HIGH), start=first, stop=False)
        pe.matmul(dst, stat(HIGH), mov(LOW), start=False, stop=False)
        return pe.matmul(dst, stat(LOW), mov(HIGH), start=False, stop=last)

    SHORT = UPS + DOWN
    half_items = (0, SHORT, SHORT + 1)

    with nc.Block() as block:

        @block.sync
        def _(sp):
            def load_x(row, i):
                sp.dma_start(x_tile[:, i, :], x[bass.ds(row, P), :]).then_inc(x_loaded[i], 16)

            for i in range(TPB):
                load_x(i * P, i)
            for m in range(WT):
                sp.dma_start(wqkv_raw[:, m, :, :], wqkv[m]).then_inc(wqkv_loaded[m], 16)
            sp.dma_start(bqk_sb[:], bqk[:, :]).then_inc(bqk_loaded, 16)
            sp.dma_start(bv_sb[:], bv[:, :]).then_inc(bv_loaded, 16)
            sp.wait_ge(wqkv_low, WT)
            sp.dma_start(wo_raw[:], wo[:, :, :]).then_inc(wo_loaded, 16)
            with sp.Fori(0, BLOCKS - 1) as b:
                for i in range(TPB):
                    sp.wait_ge(xt_ready, b * (2 * TPB) + (2 * i + 2))
                    load_x(b * BLOCK + (BLOCK + i * P), i)

            sp.wait_ge(v_low, TILES)
            sp.dma_start(bo_sb[:], bo[:, :]).then_inc(bo_loaded, 16)

            def load_item(s, slot):
                if type(s) is int and s in half_items:
                    sp.dma_start(w_raw[:, slot, 0:ITEM // 2], wffn[s, :, 0:ITEM // 2]).then_inc(w_loaded[slot], 16)
                else:
                    sp.dma_start(w_raw[:, slot, :], wffn[s, :, :]).then_inc(w_loaded[slot], 16)

            def load_residual(t):
                sp.dma_start(x_res[:], x[bass.ds(t * P, P), :]).then_inc(x_res_loaded, 16)

            def store_x1(t):
                sp.wait_ge(x1_ready, t + 1)
                sp.dma_start(x1_dram[bass.ds(t * P, P), :], x1_tile[:]).then_inc(stored, 16)

            def next_residual(t):
                sp.wait_ge(stored, t * 16 + 16)
                load_residual(t + 1)

            load_residual(0)
            load_item(0, 0)
            load_item(1, 1)
            with sp.Fori(0, TILES - TPB) as t:
                store_x1(t)
                next_residual(t)

            def load_t(b, i):
                sp.dma_start(t_tile[:, i, :], x1_dram[bass.ds(b * BLOCK + i * P, P), :]).then_inc(t_loaded[i], 16)

            def load_r(b, i):
                sp.dma_start(t_tile[:, i, :], x1_dram[bass.ds(b * BLOCK + i * P, P), :]).then_inc(r_loaded, 16)

            def tick(b, s, slot):
                sp.wait_ge(w_low, b * (2 * ITEMS) + s * 2 + 2)
                load_item((s + 2) % ITEMS if type(s) is int else s + 2, slot)

            tick(0, 0, 0)
            tick(0, 1, 1)
            sp.wait_ge(q_low, TILES)
            for i in range(TPB):
                load_t(0, i)
            with sp.Fori(TILES - TPB, TILES - 1) as t:
                store_x1(t)
                next_residual(t)
            store_x1(TILES - 1)
            sp.wait_ge(stored, 16 * TILES)

            def up(b, post):
                if post is not None:
                    sp.wait_ge(x1t_ready, b * (2 * TPB) + 2 * TPB)
                    for i in range(TPB):
                        load_r(post, i)
                    tick(b, 0, 0)
                    tick(b, 1, 1)
                if post is not None:
                    with sp.Fori(0, TPB) as i:
                        tick(b, i * 2 + 2, 0)
                        tick(b, i * 2 + 3, 1)
                        sp.wait_ge(y_added, post * TPB + i + 1)
                        sp.dma_start(out[bass.ds(post * BLOCK + i * P, P), :], y_tile[:, i, :]).then_inc(stored, 16)
                with sp.Fori(0 if post is None else TPB, FULL // 2) as p:
                    tick(b, p * 2 + 2, 0)
                    tick(b, p * 2 + 3, 1)

            def down(b, more):
                if more:
                    sp.wait_ge(x1t_ready, b * (2 * TPB) + 2 * TPB)
                    for i in range(TPB):
                        load_t(b + 1, i)
                else:
                    for i in range(TPB):
                        load_r(b, i)
                for s in range(UPS, ITEMS if more else ITEMS - 2):
                    tick(b, s, s % 2)

            up(0, None)
            with sp.Fori(0, BLOCKS - 1) as b:
                down(b, True)
                up(b + 1, b)
            down(BLOCKS - 1, False)
            row = (BLOCKS - 1) * BLOCK
            for i in range(TPB - 1):
                sp.wait_ge(y_added, (BLOCKS - 1) * TPB + i + 1)
                sp.dma_start(out[row + i * P:row + (i + 1) * P, :], y_tile[:, i, :]).then_inc(stored, 16)
            for h in range(HALF):
                sp.wait_ge(y_added, TILES + h)
                sp.dma_start(out[S - P:S, cols(h, BANK)], y_tile[:, TPB - 1, cols(h, BANK)]).then_inc(stored, 16)
            sp.wait_ge(stored, 16 * (2 * TILES + HALF - 1))

        @block.gpsimd
        def _(pool):
            pool.memset(ident[:], 0.0).then_inc(ident_cleared, 1)
            pool.memset(minus_half[:], -0.5)
            pool.memset(eps[:], EPS).then_inc(scalars_set, 1)
            pool.wait_ge(ident_cleared, 1)
            pool.affine_select(out=ident[:], in_=ident[:], compare_op=ALU.not_equal, fill=1.0, base=0,
                               pattern=[[-1, P]], channel_multiplier=1).then_inc(ident_ready, 1)
            pool.wait_ge(scalars_set, 1)

            def rstd(norm, n, i):
                pool.wait_ge(norm.moments_done, n + 1)
                pool.tensor_tensor(norm.var_eps[:, i:i + 1], norm.moments[:, i, 1:2], eps[:],
                                   ALU.add).then_inc(norm.eps_added, 1)
                pool.wait_ge(norm.eps_added, n + 1)
                pool.tensor_tensor(norm.rstd[:, i:i + 1], norm.var_eps[:, i:i + 1], minus_half[:],
                                   ALU.pow).then_inc(norm.rstd_done, 1)

            def sum_x1(t):
                pool.wait_ge(x_res_loaded, t * 16 + 16)
                pool.wait_ge(a_normed, t + 1)
                pool.tensor_tensor(x1_tile[:], x1_tile[:], x_res[:], ALU.add).then_inc(x1_ready, 1)

            def sum_y(b, i):
                pool.wait_ge(r_loaded, b * (16 * TPB) + 16 * TPB)
                pool.wait_ge(y_normed, b * TPB + i + 1)
                pool.tensor_tensor(y_tile[:, i, :], y_tile[:, i, :], t_tile[:, i, :], ALU.add).then_inc(y_added, 1)

            with pool.Fori(0, BLOCKS) as b:
                for i in range(TPB):
                    rstd(norm_x, b * TPB + i, i)
            with pool.Fori(0, TILES - 3) as t:
                rstd(norm_a, t, 0)
                sum_x1(t)
            rstd(norm_a, TILES - 3, 0)
            rstd(norm_t, 0, 0)
            rstd(norm_t, 1, 1)
            sum_x1(TILES - 3)
            rstd(norm_t, 2, 2)
            rstd(norm_t, 3, 3)
            for t in (TILES - 2, TILES - 1):
                rstd(norm_a, t, 0)
                sum_x1(t)

            def outputs(b):
                with pool.Fori(0, TPB) as i:
                    rstd(norm_y, b * TPB + i, 0)
                    sum_y(b, i)

            with pool.Fori(0, BLOCKS - 1) as b:
                for i in range(TPB):
                    rstd(norm_t, b * TPB + (TPB + i), i)
                outputs(b)
            for i in range(TPB):
                rstd(norm_y, (BLOCKS - 1) * TPB + i, i)
                if i < TPB - 2:
                    sum_y(BLOCKS - 1, i)

        @block.scalar
        def _(act):
            def split_wqkv(m):
                act.wait_ge(wqkv_loaded[m], 16)
                if m < 2 * KD:
                    dst = wqk[:, HIGH, :, cols(m)]
                else:
                    dst = wv[:, :, HIGH, cols(m - 2 * KD)]
                act.copy(dst, wqkv_raw[:, m, :, :]).then_inc(wqkv_high, 1)

            def xt_group(n, i, g):
                act.wait_ge(xt_ready, n * 2 + (g + 1))
                act.copy(xn_t[:, HIGH, 4 * g:4 * g + 4, cols(i)],
                         ps[:, 6 + g, :].rearrange("p (k t) -> p k t", k=4)).then_inc(xt_high, 1)

            def qk_out(b):
                for m in range(2 * KD):
                    act.wait_ge(qk_ready, b * (2 * KD) + (m + 1))
                    d = m % KD
                    if m < KD:
                        act.activation(q_t[:, d, cols(b, BLOCK)], ps[:, m, :], ACT.Identity,
                                       bias=bqk_sb[:, m:m + 1]).then_inc(q_copied, 1)
                    else:
                        act.activation(k_t[:, d, HIGH, cols(b, BLOCK)], ps[:, m, :], ACT.Identity,
                                       bias=bqk_sb[:, m:m + 1]).then_inc(k_high, 1)

            def v_out(n, i):
                act.wait_ge(v_summed, n + 1)
                act.copy(v[:, n, HIGH, :], v_sum[:, i % 2, :]).then_inc(v_high, 1)

            for i in range(TPB):
                xt_group(i, i, 0)
                xt_group(i, i, 1)
                if i == 1:
                    split_wqkv(0)
            for m in range(1, WT):
                split_wqkv(m)
            act.wait_ge(bqk_loaded, 16)
            with act.Fori(0, BLOCKS - 1) as b:
                qk_out(b)
                for i in range(TPB):
                    xt_group(b * TPB + (TPB + i), i, 0)
                    if i > 0:
                        v_out(b * TPB + (i - 1), i - 1)
                    xt_group(b * TPB + (TPB + i), i, 1)
                v_out(b * TPB + (TPB - 1), TPB - 1)
            act.wait_ge(wo_loaded, 16)
            act.copy(wo_sb[:, HIGH, :, :], wo_raw[:]).then_inc(wo_high, 1)
            qk_out(BLOCKS - 1)

            def q_split(t):
                if type(t) is not int or t > 0:
                    act.wait_ge(s_ready, t * 4)
                else:
                    act.wait_ge(q_copied, KD * BLOCKS)
                act.copy(q_tile[:, HIGH, :, :], q_t[:, :, cols(t)]).then_inc(q_high, 1)

            def split_item_high(b, s, slot, pair=None):
                whole = not (type(s) is int and s in half_items)
                pair = s // 2 if pair is None else pair
                act.wait_ge(w_loaded[slot], b * (16 * ITEMS // 2) + pair * 16 + 16)
                n = ITEM // 2
                if whole:
                    for p in (0, 1):
                        act.copy(w_sb[:, slot, HIGH, p * n:(p + 1) * n], w_raw[:, slot, p * n:(p + 1) * n]).then_inc(w_high, 1)
                else:
                    act.copy(w_sb[:, slot, HIGH, 0:n], w_raw[:, slot, 0:n]).then_inc(w_high, 2)

            def ot_split(t):
                act.wait_ge(ot_ready, t + 1)
                act.copy(o_t[:, HIGH, :, :], ps[:, 7, 0:D].rearrange("p (k t) -> p k t", k=KD)).then_inc(ot_high, 1)

            def pt_split(t, g, bank):
                act.wait_ge(pt_ready, t * 4 + (g + 1))
                act.copy(probs_t[:, HIGH, 4 * g:4 * g + 4, :],
                         ps[:, bank, :].rearrange("p (k t) -> p k t", k=4)).then_inc(pt_high, 1)

            def exponentials(t):
                act.wait_ge(max_negated, t + 1)
                for g in range(4):
                    act.activation(probs[:, cols(g, BANK)], ps[:, g, :], ACT.Exp, bias=neg_max[:],
                                   scale=float(D) ** -0.5, accum_out=bank_sum[:, g:g + 1]).then_inc(exp_done, 1)

            def o_out(t):
                act.wait_ge(sum_inverted, t + 1)
                act.wait_ge(pv_ready, t + 1)
                act.activation(o_half[:], ps[:, 6, D:2 * D], ACT.Copy, scale=inv_sum[:]).then_inc(o_halved, 1)

            def attend(t, item=None):
                inner = type(t) is not int
                if inner or t >= 2:
                    ot_split(t - 2)
                for g in range(4):
                    pt_split(t - 1, g, 4 + g % 2)
                if inner or t < TILES - 1:
                    q_split(t + 1)
                exponentials(t)
                if item is not None:
                    split_item_high(0, item, item)
                o_out(t - 1)

            q_split(0)
            first = (BLOCKS - 1) * TPB
            v_out(first, 0)
            q_split(1)
            exponentials(0)
            for i in range(1, TPB):
                v_out(first + i, i)
            attend(1, 0)
            attend(2, 1)
            with act.Fori(3, TILES - 1) as t:
                attend(t)
            attend(TILES - 1)

            def x1t_tile(n, i):
                for g in (0, 1):
                    act.wait_ge(x1t_ready, n * 2 + (g + 1))
                    act.copy(x1n_t[:, HIGH, 4 * g:4 * g + 4, cols(i)],
                             ps[:, 2 * (i % 2) + g, :].rearrange("p (k t) -> p k t", k=4)).then_inc(x1t_high, 1)

            last = TILES - 1
            pt_split(last, 0, 0)
            pt_split(last, 1, 1)
            ot_split(last - 1)
            pt_split(last, 2, 2)
            pt_split(last, 3, 3)
            x1t_tile(0, 0)
            x1t_tile(1, 1)
            o_out(last)
            x1t_tile(2, 2)
            x1t_tile(3, 3)

            def tick(b, s, slot, pair=None):
                act.wait_ge(item_used, b * ITEMS + s)
                if type(s) is int and s == ITEMS - 1:
                    split_item_high(b + 1, 0, 0)
                else:
                    split_item_high(b, s + 1, 1 - slot, pair)

            def silu(b, c, slot):
                act.wait_ge(gate_ready, b * FULL + c + 1)
                if type(c) is not int or c > 0:
                    act.wait_ge(prod_done, b * UPS + c)
                act.activation(silu_sb[:, slot, :], ps[:, 2 * slot, :], ACT.Silu).then_inc(silu_done, 1)

            def silu_rest(b):
                act.wait_ge(item_used, b * ITEMS + 1)
                act.activation(silu_sb[REST:P, 0, :], ps[0:REST, 0, :], ACT.Silu).then_inc(silu_done, 1)

            def up(b, first):
                if first:
                    ot_split(TILES - 1)
                else:
                    tick(b, 0, 0)
                tick(b, 1, 1)
                silu_rest(b)
                with act.Fori(0, FULL // 2) as p:
                    tick(b, p * 2 + 2, 0, p + 1)
                    silu(b, p * 2, 1)
                    tick(b, p * 2 + 3, 1, p + 2)
                    silu(b, p * 2 + 1, 0)

            def y_out(i, half, bank):
                act.copy(y_tile[:, i, cols(half, BANK)], ps[:, bank, :]).then_inc(y_copied, 1)

            def down(b, more):
                for s in range(UPS, ITEMS):
                    if s < ITEMS - 1 or more:
                        tick(b, s, s % 2)
                    if s == UPS:
                        silu(b, FULL - 1, 1)
                    if more and UPS < s <= UPS + TPB:
                        x1t_tile(b * TPB + (s - UPS - 1 + TPB), s - UPS - 1)
                    if s == SHORT + 1:
                        act.wait_ge(stored, b * (16 * TPB) + 16 * TILES)
                        for i in range(TPB):
                            y_out(i, 0, TPB + i)
                for i in range(TPB):
                    if i < TPB - 1:
                        act.wait_ge(y_ready, b * (TPB - 1) + (i + 1))
                    else:
                        act.wait_ge(item_used, b * ITEMS + ITEMS)
                    y_out(i, 1, i)

            up(0, True)
            with act.Fori(0, BLOCKS - 1) as b:
                down(b, True)
                up(b + 1, False)
            down(BLOCKS - 1, False)

        @block.vector
        def _(dve):
            def row_stats(norm, i, src):
                for h in range(HALF):
                    dve.bn_stats(norm.stats[:, i, h, :], src[:, cols(h, BANK)]).then_inc(norm.stats_done, 1)

            def stats_in(norm, n):
                dve.wait_ge(norm.stats_done, n * 2 + 2)

            def moments(norm, i):
                dve.bn_aggr(norm.moments[:, i, :], norm.stats[:, i, :, :]).then_inc(norm.moments_done, 1)

            def normed(norm, n, i, src, done):
                dve.wait_ge(norm.rstd_done, n + 1)
                dve.tensor_scalar(src, src, norm.moments[:, i, 0:1], norm.rstd[:, i:i + 1],
                                  ALU.subtract, ALU.mult).then_inc(done, 1)

            def low(dst, src, high):
                return dve.tensor_tensor(dst, src, high.bitcast(F32), ALU.subtract)

            def x_stats(i, round_):
                dve.wait_ge(x_loaded[i], round_ * 16 + 16)
                row_stats(norm_x, i, x_tile[:, i, :])

            def x_normed(n, i):
                normed(norm_x, n, i, x_tile[:, i, :], xn_done)

            def split_wqkv(m):
                dve.wait_ge(wqkv_high, m + 1)
                if m < 2 * KD:
                    low(wqk[:, LOW, :, cols(m)], wqkv_raw[:, m, :, :], wqk[:, HIGH, :, cols(m)]).then_inc(wqkv_low, 1)
                else:
                    part = cols(m - 2 * KD)
                    low(wv[:, :, LOW, part], wqkv_raw[:, m, :, :], wv[:, :, HIGH, part]).then_inc(wqkv_low, 1)

            def xt_group(n, i, g):
                dve.wait_ge(xt_high, n * 2 + (g + 1))
                k = slice(4 * g, 4 * g + 4)
                low(xn_t[:, LOW, k, cols(i)], ps[:, 6 + g, :].rearrange("p (k t) -> p k t", k=4),
                    xn_t[:, HIGH, k, cols(i)]).then_inc(xt_low, 1)

            def k_split(b):
                for d in range(KD):
                    dve.wait_ge(k_high, b * KD + (d + 1))
                    m = KD + d
                    dve.scalar_tensor_tensor(out=k_t[:, d, LOW, cols(b, BLOCK)], in0=ps[:, m, :],
                                             scalar=bqk_sb[:, m:m + 1],
                                             in1=k_t[:, d, HIGH, cols(b, BLOCK)].bitcast(F32),
                                             op0=ALU.add, op1=ALU.subtract).then_inc(k_low, 1)

            def v_add(n, i):
                dve.wait_ge(v_ready, n + 1)
                bank = ps[:, 4 + i % 2, :]
                dve.tensor_tensor(v_half[:], bank[:, D:2 * D], bv_sb[:], ALU.add).then_inc(v_halved, 1)
                dve.wait_ge(v_halved, n + 1)
                dve.tensor_tensor(v_sum[:, i % 2, :], bank[:, 0:D], v_half[:], ALU.add).then_inc(v_summed, 1)

            def v_split(n, i):
                dve.wait_ge(v_high, n + 1)
                low(v[:, n, LOW, :], v_sum[:, i % 2, :], v[:, n, HIGH, :]).then_inc(v_low, 1)

            def norm_block(b):
                x_stats(0, b)
                for i in range(1, TPB):
                    stats_in(norm_x, b * TPB + (i - 1))
                    x_stats(i, b)
                    moments(norm_x, i - 1)
                stats_in(norm_x, b * TPB + (TPB - 1))
                x_normed(b * TPB, 0)
                moments(norm_x, TPB - 1)
                for i in range(1, TPB):
                    x_normed(b * TPB + i, i)

            x_stats(0, 0)
            stats_in(norm_x, 0)
            moments(norm_x, 0)
            for i in range(1, TPB):
                x_stats(i, 0)
                stats_in(norm_x, i)
                moments(norm_x, i)
                x_normed(i - 1, i - 1)
                if i > 1:
                    xt_group(i - 2, i - 2, 0)
                    xt_group(i - 2, i - 2, 1)
            x_normed(TPB - 1, TPB - 1)
            split_wqkv(0)
            for i in (TPB - 2, TPB - 1):
                xt_group(i, i, 0)
                xt_group(i, i, 1)
            for m in range(1, WT):
                split_wqkv(m)
            dve.wait_ge(bqk_loaded, 16)
            dve.wait_ge(bv_loaded, 16)
            with dve.Fori(0, BLOCKS - 1) as b:
                norm_block(b + 1)
                k_split(b)
                for i in range(TPB):
                    xt_group(b * TPB + (TPB + i), i, 0)
                    if i > 0:
                        v_split(b * TPB + (i - 1), i - 1)
                    xt_group(b * TPB + (TPB + i), i, 1)
                    v_add(b * TPB + i, i)
                v_split(b * TPB + (TPB - 1), TPB - 1)
            dve.wait_ge(wo_high, 1)
            low(wo_sb[:, LOW, :, :], wo_raw[:], wo_sb[:, HIGH, :, :]).then_inc(wo_low, 1)
            k_split(BLOCKS - 1)

            def q_split(t):
                dve.wait_ge(q_high, t + 1)
                low(q_tile[:, LOW, :, :], q_t[:, :, cols(t)], q_tile[:, HIGH, :, :]).then_inc(q_low, 1)

            def split_item_low(b, s, slot):
                whole = not (type(s) is int and s in half_items)
                n = ITEM // 2
                for p in ((0, 1) if whole else (0,)):
                    dve.wait_ge(w_high, b * (2 * ITEMS) + s * 2 + (p + 1))
                    part = slice(p * n, (p + 1) * n)
                    low(w_sb[:, slot, LOW, part], w_raw[:, slot, part],
                        w_sb[:, slot, HIGH, part]).then_inc(w_low, 1 if whole else 2)

            def invert_sum(t):
                dve.wait_ge(exp_done, t * 4 + 4)
                dve.reduce_sum(row_sum[:], bank_sum[:], AX.X).then_inc(sum_done, 1)
                dve.wait_ge(sum_done, t + 1)
                dve.reciprocal(inv_sum[:], row_sum[:]).then_inc(sum_inverted, 1)

            def ot_split(t):
                dve.wait_ge(ot_high, t + 1)
                low(o_t[:, LOW, :, :], ps[:, 7, 0:D].rearrange("p (k t) -> p k t", k=KD),
                    o_t[:, HIGH, :, :]).then_inc(ot_low, 1)

            def maximum(t, g):
                dve.wait_ge(s_ready, t * 4 + (g + 1))
                dve.reduce_max(bank_max[:, g:g + 1], ps[:, g, :], AX.X).then_inc(bank_maxed, 1)
                if g == 3:
                    dve.wait_ge(bank_maxed, t * 4 + 4)
                    dve.reduce_max(row_max[:], bank_max[:], AX.X).then_inc(row_maxed, 1)
                    dve.wait_ge(row_maxed, t + 1)
                    dve.tensor_scalar(neg_max[:], row_max[:], -float(D) ** -0.5, None,
                                      ALU.mult).then_inc(max_negated, 1)

            def pt_split(t, g, bank):
                dve.wait_ge(pt_high, t * 4 + (g + 1))
                k = slice(4 * g, 4 * g + 4)
                low(probs_t[:, LOW, k, :], ps[:, bank, :].rearrange("p (k t) -> p k t", k=4),
                    probs_t[:, HIGH, k, :]).then_inc(pt_low, 1)

            def a_out(t, h):
                dve.wait_ge(a_ready, t * 2 + (h + 1))
                dve.tensor_tensor(x1_tile[:, cols(h, BANK)], ps[:, 4 + h, :], bo_sb[:, cols(h, BANK)],
                                  ALU.add).then_inc(a_copied, 1)

            def a_stats(t):
                dve.wait_ge(a_copied, t * 2 + 2)
                row_stats(norm_a, 0, x1_tile)
                stats_in(norm_a, t)

            def o_out(t):
                dve.wait_ge(o_halved, t + 1)
                dve.scalar_tensor_tensor(out=o_sum[:], in0=ps[:, 6, 0:D], scalar=inv_sum[:], in1=o_half[:],
                                         op0=ALU.mult, op1=ALU.add).then_inc(o_ready, 1)

            def a_norm(t):
                normed(norm_a, t, 0, x1_tile[:], a_normed)

            def t_stats(b, i):
                dve.wait_ge(t_loaded[i], b * 16 + 16)
                row_stats(norm_t, i, t_tile[:, i, :])

            def t_normed(b, i):
                normed(norm_t, b * TPB + i, i, t_tile[:, i, :], x1n_done)

            def first_block_moments(i):
                t_stats(0, i)
                stats_in(norm_t, i)
                moments(norm_t, i)

            def attend(t, item=None):
                inner = type(t) is not int
                invert_sum(t - 1)
                if inner or t >= 2:
                    ot_split(t - 2)
                for g in range(4):
                    maximum(t, g)
                    pt_split(t - 1, g, 4 + g % 2)
                if not inner and t < TILES - 1:
                    q_split(t + 1)
                if inner or t >= 2:
                    dve.wait_ge(x_res_loaded, t * 16 - 16)
                    a_out(t - 2, 0)
                    a_out(t - 2, 1)
                    a_stats(t - 2)
                    if inner:
                        q_split(t + 1)
                    moments(norm_a, 0)
                if item is not None:
                    split_item_low(0, item, item)
                if t is last:
                    first_block_moments(0)
                    first_block_moments(1)
                o_out(t - 1)
                if inner or t >= 2:
                    a_norm(t - 2)

            last = TILES - 1
            first = (BLOCKS - 1) * TPB
            q_split(0)
            v_add(first, 0)
            v_split(first, 0)
            for g in range(4):
                maximum(0, g)
            q_split(1)
            for i in range(1, TPB):
                v_add(first + i, i)
                v_split(first + i, i)
            attend(1, 0)
            dve.wait_ge(bo_loaded, 16)
            attend(2, 1)
            with dve.Fori(3, TILES - 1) as t:
                attend(t)
            attend(last)

            def x1t_tile(n, i):
                for g in (0, 1):
                    dve.wait_ge(x1t_high, n * 2 + (g + 1))
                    k = slice(4 * g, 4 * g + 4)
                    low(x1n_t[:, LOW, k, cols(i)], ps[:, 2 * (i % 2) + g, :].rearrange("p (k t) -> p k t", k=4),
                        x1n_t[:, HIGH, k, cols(i)]).then_inc(x1t_low, 1)

            def t_stats_in(b, i):
                stats_in(norm_t, b * TPB + i)

            def t_pair(b, i):
                t_stats(b, i)
                t_stats_in(b, i)
                t_stats(b, i + 1)
                moments(norm_t, i)
                t_normed(b, i)

            def t_second(b, i):
                moments(norm_t, i)
                t_normed(b, i)

            invert_sum(last)
            pt_split(last, 0, 0)
            pt_split(last, 1, 1)
            ot_split(last - 1)
            pt_split(last, 2, 2)
            pt_split(last, 3, 3)
            t_normed(0, 0)
            t_normed(0, 1)
            first_block_moments(2)
            first_block_moments(3)
            x1t_tile(0, 0)
            t_normed(0, 2)
            x1t_tile(1, 1)
            t_normed(0, 3)
            o_out(last)
            x1t_tile(2, 2)
            x1t_tile(3, 3)
            dve.wait_ge(x_res_loaded, last * 16)
            a_out(last - 1, 0)
            a_out(last - 1, 1)
            a_stats(last - 1)
            moments(norm_a, 0)
            a_norm(last - 1)

            def tick(b, s, slot):
                if type(s) is int and s == ITEMS - 1:
                    split_item_low(b + 1, 0, 0)
                else:
                    split_item_low(b, s + 1, 1 - slot)

            def hidden(b, c, slot):
                dve.wait_ge(h_low, b * UPS + c + 1)
                dve.wait_ge(silu_done, b * UPS + c + 2)
                dve.wait_ge(item_used, b * ITEMS + c + 2)
                dve.tensor_tensor(h_f32[:], silu_sb[:, slot, :], ps[:, 2 * slot + 1, :], ALU.mult).then_inc(prod_done, 1)
                dve.wait_ge(prod_done, b * UPS + c + 2)
                dve.tensor_copy(h_t[:, c, HIGH, :], h_f32[:]).then_inc(h_high, 1)
                dve.wait_ge(h_high, b * UPS + c + 2)
                low(h_t[:, c, LOW, :], h_f32[:], h_t[:, c, HIGH, :]).then_inc(h_low, 1)

            def hidden_rest(b):
                up_half = slice(REST, P)
                dve.wait_ge(silu_done, b * UPS + 1)
                dve.tensor_tensor(h_f32[up_half, :], silu_sb[up_half, 0, :], ps[up_half, 0, :],
                                  ALU.mult).then_inc(prod_done, 1)
                dve.wait_ge(prod_done, b * UPS + 1)
                dve.tensor_copy(h_rest[0:REST, :], h_f32[up_half, :])
                dve.tensor_copy(h_rest[up_half, :], h_f32[up_half, :]).then_inc(h_high, 1)
                dve.wait_ge(h_high, b * UPS + 1)
                low(h_rest[up_half, :], h_f32[up_half, :], h_rest[up_half, :]).then_inc(h_low, 1)

            def y_stats(b, i):
                dve.wait_ge(y_copied, b * (2 * TPB) + i + (TPB + 1))
                row_stats(norm_y, 0, y_tile[:, i, :])

            def y_norm(b, i):
                normed(norm_y, b * TPB + i, 0, y_tile[:, i, :], y_normed)

            def up(b, post):
                if post is None:
                    ot_split(last)
                else:
                    tick(b, 0, 0)
                tick(b, 1, 1)
                hidden_rest(b)
                if post is None:
                    dve.wait_ge(x_res_loaded, TILES * 16)
                    a_out(last, 0)
                    a_out(last, 1)
                    a_stats(last)
                    moments(norm_a, 0)
                    a_norm(last)
                else:
                    with dve.Fori(0, TPB) as i:
                        tick(b, i * 2 + 2, 0)
                        hidden(b, i * 2, 1)
                        y_stats(post, i)
                        stats_in(norm_y, post * TPB + i)
                        tick(b, i * 2 + 3, 1)
                        moments(norm_y, 0)
                        hidden(b, i * 2 + 1, 0)
                        y_norm(post, i)
                with dve.Fori(0 if post is None else TPB, FULL // 2) as p:
                    tick(b, p * 2 + 2, 0)
                    hidden(b, p * 2, 1)
                    tick(b, p * 2 + 3, 1)
                    hidden(b, p * 2 + 1, 0)

            def down(b, more):
                for s in range(UPS, ITEMS):
                    if more and s in (UPS + 1, UPS + 3):
                        t_stats_in(b + 1, s - UPS)
                    if s < ITEMS - 1 or more:
                        tick(b, s, s % 2)
                    if s == UPS:
                        hidden(b, FULL - 1, 1)
                    if more and s in (UPS, UPS + 2):
                        t_pair(b + 1, s - UPS)
                    if more and s in (UPS + 1, UPS + 3):
                        t_second(b + 1, s - UPS)
                    if more and UPS < s <= UPS + TPB:
                        x1t_tile(b * TPB + (s - UPS - 1 + TPB), s - UPS - 1)
                    if not more and s == ITEMS - 2:
                        dve.wait_ge(y_copied, b * (2 * TPB) + TPB)
                        for i in range(TPB):
                            dve.bn_stats(norm_y.stats[:, i, 0, :], y_tile[:, i, 0:BANK]).then_inc(norm_y.stats_done, 1)

            up(0, None)
            with dve.Fori(0, BLOCKS - 1) as b:
                down(b, True)
                up(b + 1, b)
            down(BLOCKS - 1, False)
            b = BLOCKS - 1

            def last_moments(i):
                dve.wait_ge(y_copied, b * (2 * TPB) + TPB + i + 1)
                dve.bn_stats(norm_y.stats[:, i, 1, :], y_tile[:, i, BANK:C]).then_inc(norm_y.stats_done, 1)
                dve.wait_ge(norm_y.stats_done, b * (2 * TPB) + TPB + i + 1)
                moments(norm_y, i)

            def last_normed(i, part):
                dve.wait_ge(norm_y.rstd_done, b * TPB + i + 1)
                dve.tensor_scalar(y_tile[:, i, part], y_tile[:, i, part], norm_y.moments[:, i, 0:1],
                                  norm_y.rstd[:, i:i + 1], ALU.subtract, ALU.mult).then_inc(y_normed, 1)

            def last_sum(i, part, done):
                dve.wait_ge(y_normed, b * TPB + done)
                dve.tensor_tensor(y_tile[:, i, part], y_tile[:, i, part], t_tile[:, i, part],
                                  ALU.add).then_inc(y_added, 1)

            whole = slice(0, C)
            for i in range(TPB - 1):
                last_moments(i)
                last_normed(i, whole)
            last_moments(TPB - 1)
            dve.wait_ge(r_loaded, BLOCKS * 16 * TPB)
            dve.wait_ge(y_added, b * TPB + TPB - 2)
            last_sum(TPB - 2, whole, TPB - 1)
            for h in range(HALF):
                last_normed(TPB - 1, cols(h, BANK))
            for h in range(HALF):
                last_sum(TPB - 1, cols(h, BANK), TPB + h)

        @block.tensor
        def _(pe):
            pe.wait_ge(ident_ready, 1)

            def transposes(bank, k0, src, count):
                for j in range(count):
                    last = pe.transpose(ps[:, bank, cols(j)], src[:, cols(k0 + j)], ident[:])
                return last

            def xt_group(n, i, g):
                if g == 0:
                    pe.wait_ge(xn_done, n + 1)
                if i > 0:
                    pe.wait_ge(xt_low, n * 2 + (g - 1))
                transposes(6 + g, 4 * g, x_tile[:, i, :], 4).then_inc(xt_ready, 1)

            def qk(b):
                for m in range(2 * KD):
                    pe.wait_ge(wqkv_low, m + 1)
                    for k in range(KC):
                        if m == 0 and k % 4 == 0:
                            pe.wait_ge(xt_low, b * (2 * TPB) + (2 * TPB - 1 + k // 4))
                        last = three(pe, ps[:, m, :], lambda p: wqk[:, p, k, cols(m)], lambda p: xn_t[:, p, k, :],
                                     k == 0, k == KC - 1)
                    last.then_inc(qk_ready, 1)

            def project_v(n, i, then):
                bank = ps[:, 4 + i % 2, :]
                if i > 1 or type(n) is int:
                    pe.wait_ge(v_summed, n - 1)
                for k in range(KC):
                    pe.matmul(bank, xn_t[:, HIGH, k, cols(i)], wv[:, k, :, :], start=k == 0, stop=False)
                    last = pe.matmul(bank[:, 0:D], xn_t[:, LOW, k, cols(i)], wv[:, k, HIGH, :],
                                     start=False, stop=k == KC - 1)
                    if k == KC - 1:
                        last.then_inc(v_ready, 1)
                    if k % 4 == 3:
                        then(k // 4)

            for i in range(TPB):
                xt_group(i, i, 0)
                xt_group(i, i, 1)
            with pe.Fori(0, BLOCKS - 1) as b:
                qk(b)
                pe.wait_ge(wqkv_low, WT)
                for i in range(TPB):
                    project_v(b * TPB + i, i, lambda g: xt_group(b * TPB + (TPB + i), i, g))
            qk(BLOCKS - 1)

            def scores(t, g):
                for d in range(KD):
                    last = three(pe, ps[:, g, :], lambda p: q_tile[:, p, d, :],
                                 lambda p: k_t[:, d, p, cols(g, BANK)], d == 0, d == KD - 1)
                last.then_inc(s_ready, 1)

            def transpose_probs(g, bank):
                transposes(bank, 4 * g, probs, 4).then_inc(pt_ready, 1)

            def transpose_output(t):
                pe.wait_ge(o_ready, t + 1)
                transposes(7, 0, o_sum, KD).then_inc(ot_ready, 1)

            def project_output(h):
                for d in range(KD):
                    last = three(pe, ps[:, 4 + h, :], lambda p: o_t[:, p, d, :],
                                 lambda p: wo_sb[:, p, d, cols(h, BANK)], d == 0, d == KD - 1)
                last.then_inc(a_ready, 1)

            def weigh(t, g):
                pe.wait_ge(pt_low, t * 4 + (g + 1))
                for k in range(4 * g, 4 * g + 4):
                    pe.matmul(ps[:, 6, :], probs_t[:, HIGH, k, :], v[:, k, :, :], start=k == 0, stop=False)
                    last = pe.matmul(ps[:, 6, 0:D], probs_t[:, LOW, k, :], v[:, k, HIGH, :],
                                     start=False, stop=k == TILES - 1)
                if g == 3:
                    last.then_inc(pv_ready, 1)

            def attend(t):
                older = type(t) is not int or t >= 2
                pe.wait_ge(q_low, t + 1)
                for g in range(4):
                    pe.wait_ge(exp_done, t * 4 + (g - 3))
                    scores(t, g)
                    if older and g == 0:
                        transpose_output(t - 2)
                    if g > 1:
                        pe.wait_ge(pt_low, t * 4 + (g - 5))
                    transpose_probs(g, 4 + g % 2)
                if older:
                    pe.wait_ge(ot_low, t - 1)
                    for h in range(HALF):
                        pe.wait_ge(pt_low, t * 4 + (h - 1))
                        project_output(h)
                for g in range(4):
                    weigh(t - 1, g)

            first = (BLOCKS - 1) * TPB
            nothing = lambda g: None
            project_v(first, 0, nothing)
            pe.wait_ge(k_low, KD * BLOCKS)
            pe.wait_ge(q_low, 1)
            for g in range(4):
                scores(0, g)
            for i in range(1, TPB):
                project_v(first + i, i, nothing)
            pe.wait_ge(v_low, TILES)
            attend(1)
            pe.wait_ge(wo_low, 1)
            with pe.Fori(2, TILES) as t:
                attend(t)

            def x1t_tile(n, i):
                pe.wait_ge(x1n_done, n + 1)
                for g in (0, 1):
                    if i > 1:
                        pe.wait_ge(x1t_low, n * 2 + (g - 3))
                    transposes(2 * (i % 2) + g, 4 * g, t_tile[:, i, :], 4).then_inc(x1t_ready, 1)

            last_tile = TILES - 1
            for g in range(4):
                pe.wait_ge(exp_done, 4 * last_tile + 4)
                transpose_probs(g, g)
                if g == 1:
                    transpose_output(last_tile - 1)
            for g in range(4):
                weigh(last_tile, g)
            x1t_tile(0, 0)
            x1t_tile(1, 1)
            pe.wait_ge(ot_low, last_tile)
            project_output(0)
            project_output(1)
            x1t_tile(2, 2)
            x1t_tile(3, 3)

            def up(b, post):
                pe.wait_ge(x1t_low, b * (2 * TPB) + 2 * TPB)
                if post is not None:
                    pe.wait_ge(y_copied, post * (2 * TPB) + (TPB + 1))
                pe.wait_ge(w_low, b * (2 * ITEMS) + 2)
                for k in range(KC):
                    last = three(pe, ps[:, 0, :], lambda p: w_sb[:, 0, p, cols(k)], lambda p: x1n_t[:, p, k, :],
                                 k == 0, k == KC - 1)
                last.then_inc(item_used, 1)
                if post is None:
                    transpose_output(last_tile)

                def gate_up(c, slot, older):
                    if older:
                        pe.wait_ge(prod_done, b * UPS + c)
                    for part in (0, 1):
                        pe.wait_ge(w_low, b * (2 * ITEMS) + c * 2 + (part + 3))
                        for k in range(KC):
                            last = three(pe, ps[:, 2 * slot + part, :],
                                         lambda p: w_sb[:, slot, p, cols(part * KC + k)],
                                         lambda p: x1n_t[:, p, k, :], k == 0, k == KC - 1)
                        last.then_inc(item_used if part else gate_ready, 1)

                if post is not None:
                    pe.wait_ge(y_copied, post * (2 * TPB) + 2 * TPB)
                gate_up(0, 1, False)
                if post is None:
                    pe.wait_ge(ot_low, TILES)
                    pe.wait_ge(a_copied, HALF * last_tile)
                    project_output(0)
                    project_output(1)
                with pe.Fori(0, FULL // 2) as p:
                    gate_up(p * 2 + 1, 0, True)
                    gate_up(p * 2 + 2, 1, True)

            def down(b, more):
                def add_chunk(bank, i, c, w, first):
                    return three(pe, ps[:, bank, :], lambda p: h_t[:, c, p, cols(i)], w, first, False)

                def full_item(s, j, bank0, first, last):
                    slot = s % 2
                    pe.wait_ge(w_low, b * (2 * ITEMS) + (2 * s + 2))
                    for i in range(TPB):
                        for q in range(CPI):
                            c = CPI * j + q
                            mm = three(pe, ps[:, bank0 + i, :], lambda p: h_t[:, c, p, cols(i)],
                                       lambda p: w_sb[:, slot, p, cols(q, BANK)],
                                       first and q == 0, last and q == CPI - 1)
                        if last and i < TPB - 1:
                            mm.then_inc(y_ready, 1)
                    mm.then_inc(item_used, 1)

                def short_item(s, bank0, first, last):
                    slot = s % 2
                    pe.wait_ge(w_low, b * (2 * ITEMS) + (2 * s + 2))
                    for i in range(TPB):
                        three(pe, ps[:, bank0 + i, :], lambda p: h_t[:, FULL - 1, p, cols(i)],
                              lambda p: w_sb[:, slot, p, cols(0, BANK)], first, False)
                        for p in (HIGH, LOW):
                            mm = pe.matmul(ps[:, bank0 + i, :], h_rest[:, cols(i)], w_sb[:, slot, p, cols(1, BANK)],
                                           start=False, stop=last and p == LOW)
                    mm.then_inc(item_used, 1)

                for j in range(DOWN):
                    if more and j > 0:
                        if j == 1:
                            pe.wait_ge(prod_done, b * UPS + UPS)
                        x1t_tile(b * TPB + (TPB + j - 1), j - 1)
                    pe.wait_ge(h_low, b * UPS + (CPI * (j + 1) + 1))
                    full_item(UPS + j, j, TPB, j == 0, False)
                pe.wait_ge(h_low, b * UPS + UPS)
                short_item(SHORT, TPB, False, True)
                if more:
                    pe.wait_ge(x1t_low, b * (2 * TPB) + 4 * TPB)
                short_item(SHORT + 1, 0, True, False)
                for j in range(DOWN):
                    full_item(SHORT + 2 + j, j, 0, False, j == DOWN - 1)

            up(0, None)
            with pe.Fori(0, BLOCKS - 1) as b:
                down(b, True)
                up(b + 1, b)
            down(BLOCKS - 1, False)


def kernel(**inputs):
    import numpy as np
    import concourse.bacc as bacc
    from concourse.bass_utils import run_bass_kernel_spmd

    def chunks(a):
        return a.reshape(a.shape[0] // P, P, a.shape[1]).transpose(1, 0, 2)

    a = {name: np.asarray(value) for name, value in inputs.items()}
    bqkv = a["L0_attn_bqkv"]
    gate, up, down = a["L0_ffn_W_gate"].T, a["L0_ffn_W_up"].T, a["L0_ffn_W_down"].T
    short = UPS + DOWN
    wffn = np.zeros((ITEMS, P, ITEM), a["L0_ffn_W_gate"].dtype)
    wffn[0, :, 0:KC * P] = chunks(np.concatenate([gate[:, FULL * P:], up[:, FULL * P:]], 1)).reshape(P, -1)
    for c in range(FULL):
        f = slice(c * P, (c + 1) * P)
        wffn[1 + c, :, 0:KC * P] = chunks(gate[:, f]).reshape(P, -1)
        wffn[1 + c, :, KC * P:] = chunks(up[:, f]).reshape(P, -1)
    for h in range(HALF):
        part = down[:, h * BANK:(h + 1) * BANK]
        first = short + 2 if h else UPS
        for j in range(DOWN):
            wffn[first + j] = chunks(part[j * CPI * P:(j + 1) * CPI * P]).reshape(P, -1)
        wffn[short + h, :, 0:BANK] = part[(FULL - 1) * P:FULL * P]
        wffn[short + h, 0:REST, BANK:2 * BANK] = part[FULL * P:]
        wffn[short + h, REST:P, BANK:2 * BANK] = part[FULL * P:]

    arrays = {
        "x": a["L0_attn_x"].reshape(S, C),
        "wqkv": np.stack([chunks(a["L0_attn_Wqkv"][:, m * P:(m + 1) * P]) for m in range(WT)]),
        "bqk": bqkv[0:2 * D].reshape(2 * KD, P).T,
        "bv": np.broadcast_to(bqkv[2 * D:], (P, D)),
        "wo": chunks(a["L0_attn_Wo"]),
        "bo": np.broadcast_to(a["L0_attn_bo"], (P, C)),
        "wffn": wffn,
    }
    arrays = {name: np.ascontiguousarray(value) for name, value in arrays.items()}
    nc = bacc.Bacc("TRN2", target_bir_lowering=False, num_devices=1)
    args = [nc.dram_tensor(name, value.shape, mybir.dt.from_np(value.dtype), kind="ExternalInput").ap()
            for name, value in arrays.items()]
    args.append(nc.dram_tensor("out", (S, C), F32, kind="ExternalOutput").ap())
    transformer_block(nc, *args)
    result = run_bass_kernel_spmd(nc, [arrays], core_ids=[0])
    return result.results[0]["out"].reshape(a["L0_attn_x"].shape)
```

```python
import concourse.bass as bass
from concourse import mybir

F32 = mybir.dt.float32
F32R = mybir.dt.float32r
ACT = mybir.ActivationFunctionType
ALU = mybir.AluOpType
AX = mybir.AxisListType

P = 128
S = 2048
C = 1024
D = 256
F = 2752
EPS = 1e-5
BANK = 512
KC = C // P
KD = D // P
WT = 3 * KD
TILES = S // P
BLOCK = 512
TPB = BLOCK // P
BLOCKS = S // BLOCK
FULL = F // P
REST = F - FULL * P
HALF = C // BANK
ITEM = 2048
CPI = ITEM // BANK
DOWN = (FULL - 1) // CPI
UPS = FULL + 1
ITEMS = UPS + HALF * (DOWN + 1)
POOL_K = 3
DVE_K = KC - POOL_K
HIGH, LOW = 0, 1
assert 2 * REST == P and FULL == CPI * DOWN + 1 and ITEMS % 2 == 0


def transformer_block(nc, x, xt, wqkv, bqk, bv, wo, bo, wffn, out):
    KB = 1024
    base = -(-nc.sbuf_base // 64) * 64

    def at(name, kb, shape, dt=F32):
        return nc.alloc_sbuf_tensor_at(name, [P] + shape, dt, offset=base + int(kb * KB))

    q_t = at("q_t", 0, [KD, S])
    k_t = at("k_t", 16, [KD, 2, S], F32R)
    v = at("v", 48, [TILES, 2, D], F32R)
    xn_t = at("xn_t", 80, [2, KC, BLOCK], F32R)
    rows_first = at("rows_first", 0, [TPB, C])
    x_tile = at("x_tile", 16, [TPB, C])
    wqkv_raw = at("wqkv_raw", 48, [WT, KC, P])
    xt_f32 = at("xt_f32", 112, [KC, BLOCK])
    norm_rows = at("norm_rows", 128, [2, BLOCK])
    x_rows = at("x_rows", 136, [TPB, C])
    v_half = at("v_half", 152, [D])
    v_sum = at("v_sum", 153, [2, D])
    bv_sb = at("bv_sb", 155, [D])
    wqk = at("wqk", 156, [2, KC, 2 * D], F32R)
    wv = at("wv", 188, [KC, 2, D], F32R)
    probs_t = at("probs_t", 80, [2, TILES, P], F32R)
    x1_tile = at("x1_tile", 96, [C])
    x_res = at("x_res", 100, [C])
    bo_sb = at("bo_sb", 104, [C])
    wo_sb = at("wo_sb", 112, [2, KD, C], F32R)
    wo_raw = at("wo_raw", 128, [KD, C])
    probs = at("probs", 136, [S])
    q_tile = at("q_tile", 144, [2, KD, P], F32R)
    o_half = at("o_half", 146, [D])
    o_sum = at("o_sum", 147, [D])
    o_t = at("o_t", 108, [2, KD, P], F32R)
    t_tile = at("t_tile", 0, [TPB, C])
    x1n_t = at("x1n_t", 16, [2, KC, BLOCK], F32R)
    y_tile = at("y_tile", 48, [TPB, C])
    h_t = at("h_t", 64, [FULL, 2, BLOCK], F32R)
    h_rest = at("h_rest", 64 + 4 * FULL, [BLOCK], F32R)
    silu_sb = at("silu_sb", 150, [2, BLOCK])
    h_f32 = at("h_f32", 154, [BLOCK])
    w_raw = at("w_raw", 156, [2, ITEM])
    w_sb = at("w_sb", 172, [2, 2, ITEM], F32R)
    ident = at("ident", 204, [P])
    small = [204.5]

    def tiny(name, shape):
        size = 4
        for n in shape:
            size *= n
        t = at(name, small[0], shape)
        small[0] += -(-size // 32) * 32 / KB
        return t

    bqk_sb = tiny("bqk_sb", [2 * KD])
    minus_half = tiny("minus_half", [1])
    eps = tiny("eps", [1])
    bank_max = tiny("bank_max", [4])
    row_max = tiny("row_max", [1])
    neg_max = tiny("neg_max", [1])
    bank_sum = tiny("bank_sum", [4])
    row_sum = tiny("row_sum", [1])
    inv_sum = tiny("inv_sum", [1])

    ps = nc.alloc_psum_tensor("ps", [P, 8, BANK], F32)
    x1_dram = nc.dram_tensor("x1_dram", [S, C], F32)
    stats_dram = nc.dram_tensor("stats_dram", [BLOCKS, 2, BLOCK], F32)

    sem = nc.alloc_semaphore

    class Norm:

        def __init__(self, name, places):
            self.places = places
            self.stats = tiny(name + "_stats", [places, 2, 6])
            self.moments = tiny(name + "_moments", [2, places])
            self.var_eps = tiny(name + "_var_eps", [places])
            self.rstd = tiny(name + "_rstd", [places])
            self.stats_done = sem(name + "_stats_done")
            self.moments_done = sem(name + "_moments_done")
            self.eps_added = sem(name + "_eps_added")
            self.rstd_done = sem(name + "_rstd_done")

    norm_x = Norm("norm_x", TPB)
    norm_a = Norm("norm_a", 1)
    norm_t = Norm("norm_t", TPB)
    norm_y = Norm("norm_y", TPB)

    ident_cleared, ident_ready, scalars_set = sem("ident_cleared"), sem("ident_ready"), sem("scalars_set")
    bqk_loaded, bv_loaded, bo_loaded = sem("bqk_loaded"), sem("bv_loaded"), sem("bo_loaded")
    wqkv_loaded = [sem(f"wqkv_loaded{m}") for m in range(WT)]
    wqkv_high, wqk_low, wv_low = sem("wqkv_high"), sem("wqk_low"), sem("wv_low")
    wo_loaded, wo_high, wo_low = sem("wo_loaded"), sem("wo_high"), sem("wo_low")
    x_half_loaded = [sem(f"x_half_loaded{h}") for h in range(HALF)]
    x_loaded = [sem(f"x_loaded{i}") for i in range(1, TPB)]
    xn_done, xt_ready, xt_high, xt_low = sem("xn_done"), sem("xt_ready"), sem("xt_high"), sem("xt_low")
    rows_first_loaded, rows_loaded, xt_loaded = sem("rows_first_loaded"), sem("rows_loaded"), sem("xt_loaded")
    stats_stored, norm_rows_loaded = sem("stats_stored"), sem("norm_rows_loaded")
    xt_centred, xt_normed, v_halfway = sem("xt_centred"), sem("xt_normed"), sem("v_halfway")
    xt_centred_pool, xt_normed_pool = sem("xt_centred_pool"), sem("xt_normed_pool")
    qk_ready, q_copied, k_high, k_low = sem("qk_ready"), sem("q_copied"), sem("k_high"), sem("k_low")
    v_ready, v_halved, v_summed = sem("v_ready"), sem("v_halved"), sem("v_summed")
    v_high, v_low = sem("v_high"), sem("v_low")
    q_high, q_low, s_ready = sem("q_high"), sem("q_low"), sem("s_ready")
    bank_maxed, row_maxed, max_negated = sem("bank_maxed"), sem("row_maxed"), sem("max_negated")
    exp_done, sum_done, sum_inverted = sem("exp_done"), sem("sum_done"), sem("sum_inverted")
    pt_ready, pt_high, pt_low = sem("pt_ready"), sem("pt_high"), sem("pt_low")
    pv_ready, o_halved, o_ready = sem("pv_ready"), sem("o_halved"), sem("o_ready")
    ot_ready, ot_high, ot_low = sem("ot_ready"), sem("ot_high"), sem("ot_low")
    a_ready, a_copied, a_normed = sem("a_ready"), sem("a_copied"), sem("a_normed")
    x_res_loaded, x1_ready = sem("x_res_loaded"), sem("x1_ready")
    stored = sem("stored")
    w_loaded = [sem("w_loaded0"), sem("w_loaded1")]
    w_high, w_low, item_used = sem("w_high"), sem("w_low"), sem("item_used")
    t_loaded = [sem(f"t_loaded{i}") for i in range(TPB)]
    r_loaded = sem("r_loaded")
    x1n_done, x1t_ready = sem("x1n_done"), sem("x1t_ready")
    x1t_high, x1t_low = sem("x1t_high"), sem("x1t_low")
    gate_ready, silu_done, prod_done = sem("gate_ready"), sem("silu_done"), sem("prod_done")
    h_high, h_low, rest_split = sem("h_high"), sem("h_low"), sem("rest_split")
    y_ready, y_copied, y_normed, y_added = sem("y_ready"), sem("y_copied"), sem("y_normed"), sem("y_added")

    def cols(i, width=P):
        return bass.ds(i * width, width) if type(i) is not int else slice(i * width, (i + 1) * width)

    def three(pe, dst, stat, mov, first, last):
        pe.matmul(dst, stat(HIGH), mov(HIGH), start=first, stop=False)
        pe.matmul(dst, stat(HIGH), mov(LOW), start=False, stop=False)
        return pe.matmul(dst, stat(LOW), mov(HIGH), start=False, stop=last)

    SHORT = UPS + DOWN
    half_items = (0, SHORT, SHORT + 1)

    with nc.Block() as block:

        @block.sync
        def _(sp):
            for h in range(HALF):
                sp.dma_start(x_tile[:, 0, cols(h, BANK)], x[0:P, cols(h, BANK)]).then_inc(x_half_loaded[h], 16)
            for i in range(1, TPB):
                sp.dma_start(x_tile[:, i, :], x[i * P:(i + 1) * P, :]).then_inc(x_loaded[i - 1], 16)

            def load_rows(b, dst, loaded):
                rows = x[b * BLOCK:(b + 1) * BLOCK, :].rearrange("(p i) c -> p i c", i=TPB)
                sp.dma_start(dst[:], rows).then_inc(loaded, 16)

            def load_wqkv(m):
                sp.dma_start(wqkv_raw[:, m, :, :], wqkv[m]).then_inc(wqkv_loaded[m], 16)

            def store_stats(b):
                sp.wait_ge(norm_x.rstd_done, b * TPB + TPB)
                for part, stat in ((0, norm_x.moments[:, 0, :]), (1, norm_x.rstd[:, :])):
                    sp.dma_start(stats_dram[b, part, :].rearrange("(p i) -> p i", i=TPB),
                                 stat).then_inc(stats_stored, 16)

            def block_normed(b):
                sp.wait_ge(xt_normed, b * DVE_K)
                sp.wait_ge(xt_normed_pool, b * POOL_K)

            def load_norm_rows(b):
                sp.wait_ge(stats_stored, b * 32)
                sp.dma_start(norm_rows[:], stats_dram[b].partition_broadcast(P)).then_inc(norm_rows_loaded, 16)

            def load_transposed(b, h):
                k = cols(h, KC // 2)
                sp.dma_start(xt_f32[:, k, :], xt[b, :, k, :]).then_inc(xt_loaded, 16)

            load_wqkv(0)
            load_wqkv(1)
            load_rows(1, rows_first, rows_first_loaded)
            sp.dma_start(bqk_sb[:], bqk[:, :]).then_inc(bqk_loaded, 16)
            sp.dma_start(bv_sb[:], bv[:, :]).then_inc(bv_loaded, 16)
            for m in range(2, WT):
                load_wqkv(m)
            load_rows(2, x_rows, rows_loaded)
            load_transposed(1, 0)
            store_stats(1)
            load_transposed(1, 1)
            load_norm_rows(1)
            for b in range(2, BLOCKS):
                store_stats(b)
                block_normed(b - 1)
                load_norm_rows(b)
                if b < BLOCKS - 1:
                    load_rows(b + 1, x_rows, rows_loaded)
                sp.wait_ge(xt_low, b * (2 * TPB))
                for h in (0, 1):
                    load_transposed(b, h)
            block_normed(BLOCKS - 1)
            sp.dma_start(wo_raw[:], wo[:, :, :]).then_inc(wo_loaded, 16)

            sp.wait_ge(v_low, TILES)
            sp.dma_start(bo_sb[:], bo[:, :]).then_inc(bo_loaded, 16)

            def load_item(s, slot):
                if type(s) is int and s in half_items:
                    sp.dma_start(w_raw[:, slot, 0:ITEM // 2], wffn[s, :, 0:ITEM // 2]).then_inc(w_loaded[slot], 16)
                else:
                    sp.dma_start(w_raw[:, slot, :], wffn[s, :, :]).then_inc(w_loaded[slot], 16)

            def load_residual(t):
                sp.dma_start(x_res[:], x[bass.ds(t * P, P), :]).then_inc(x_res_loaded, 16)

            def store_x1(t):
                sp.wait_ge(x1_ready, t + 1)
                sp.dma_start(x1_dram[bass.ds(t * P, P), :], x1_tile[:]).then_inc(stored, 16)

            def next_residual(t):
                sp.wait_ge(stored, t * 16 + 16)
                load_residual(t + 1)

            load_residual(0)
            load_item(0, 0)
            load_item(1, 1)
            with sp.Fori(0, TILES - TPB) as t:
                store_x1(t)
                next_residual(t)

            def load_t(b, i):
                sp.dma_start(t_tile[:, i, :], x1_dram[bass.ds(b * BLOCK + i * P, P), :]).then_inc(t_loaded[i], 16)

            def load_r(b, i):
                sp.dma_start(t_tile[:, i, :], x1_dram[bass.ds(b * BLOCK + i * P, P), :]).then_inc(r_loaded, 16)

            def tick(b, s, slot):
                sp.wait_ge(w_low, b * (2 * ITEMS) + s * 2 + 2)
                load_item((s + 2) % ITEMS if type(s) is int else s + 2, slot)

            tick(0, 0, 0)
            tick(0, 1, 1)
            sp.wait_ge(q_low, TILES)
            for i in range(TPB):
                load_t(0, i)
            with sp.Fori(TILES - TPB, TILES - 1) as t:
                store_x1(t)
                next_residual(t)
            store_x1(TILES - 1)
            sp.wait_ge(stored, 16 * TILES)

            def up(b, post):
                if post is not None:
                    sp.wait_ge(x1t_ready, b * (2 * TPB) + 2 * TPB)
                    for i in range(TPB):
                        load_r(post, i)
                    tick(b, 0, 0)
                    tick(b, 1, 1)
                if post is not None:
                    with sp.Fori(0, TPB) as i:
                        tick(b, i * 2 + 2, 0)
                        tick(b, i * 2 + 3, 1)
                        sp.wait_ge(y_added, post * TPB + i + 1)
                        sp.dma_start(out[bass.ds(post * BLOCK + i * P, P), :], y_tile[:, i, :]).then_inc(stored, 16)
                with sp.Fori(0 if post is None else TPB, FULL // 2) as p:
                    tick(b, p * 2 + 2, 0)
                    tick(b, p * 2 + 3, 1)

            def down(b, more):
                if more:
                    sp.wait_ge(x1t_ready, b * (2 * TPB) + 2 * TPB)
                    for i in range(TPB):
                        load_t(b + 1, i)
                else:
                    for i in range(TPB):
                        load_r(b, i)
                for s in range(UPS, ITEMS if more else ITEMS - 2):
                    tick(b, s, s % 2)

            up(0, None)
            with sp.Fori(0, BLOCKS - 1) as b:
                down(b, True)
                up(b + 1, b)
            down(BLOCKS - 1, False)
            row = (BLOCKS - 1) * BLOCK
            for i in range(TPB - 1):
                sp.wait_ge(y_added, (BLOCKS - 1) * TPB + i + 1)
                sp.dma_start(out[row + i * P:row + (i + 1) * P, :], y_tile[:, i, :]).then_inc(stored, 16)
            for h in range(HALF):
                sp.wait_ge(y_added, TILES + h)
                sp.dma_start(out[S - P:S, cols(h, BANK)], y_tile[:, TPB - 1, cols(h, BANK)]).then_inc(stored, 16)
            sp.wait_ge(stored, 16 * (2 * TILES + HALF - 1))

        @block.gpsimd
        def _(pool):
            pool.memset(ident[:], 0.0).then_inc(ident_cleared, 1)
            pool.memset(minus_half[:], -0.5)
            pool.memset(eps[:], EPS).then_inc(scalars_set, 1)
            pool.wait_ge(ident_cleared, 1)
            pool.affine_select(out=ident[:], in_=ident[:], compare_op=ALU.not_equal, fill=1.0, base=0,
                               pattern=[[-1, P]], channel_multiplier=1).then_inc(ident_ready, 1)
            pool.wait_ge(scalars_set, 1)

            def rstd(norm, n, i):
                pool.wait_ge(norm.moments_done, n + 1)
                pool.tensor_tensor(norm.var_eps[:, i:i + 1], norm.moments[:, 1, i:i + 1], eps[:],
                                   ALU.add).then_inc(norm.eps_added, 1)
                pool.wait_ge(norm.eps_added, n + 1)
                pool.tensor_tensor(norm.rstd[:, i:i + 1], norm.var_eps[:, i:i + 1], minus_half[:],
                                   ALU.pow).then_inc(norm.rstd_done, 1)

            def sum_x1(t):
                pool.wait_ge(x_res_loaded, t * 16 + 16)
                pool.wait_ge(a_normed, t + 1)
                pool.tensor_tensor(x1_tile[:], x1_tile[:], x_res[:], ALU.add).then_inc(x1_ready, 1)

            def sum_y(b, i):
                pool.wait_ge(r_loaded, b * (16 * TPB) + 16 * TPB)
                pool.wait_ge(y_normed, b * TPB + i + 1)
                pool.tensor_tensor(y_tile[:, i, :], y_tile[:, i, :], t_tile[:, i, :], ALU.add).then_inc(y_added, 1)

            def norm_share(b):
                pool.wait_ge(xt_loaded, b * 32)
                pool.wait_ge(norm_rows_loaded, b * 16)
                for j in range(POOL_K):
                    k = DVE_K + j
                    pool.tensor_tensor(xt_f32[:, k, :], xt_f32[:, k, :], norm_rows[:, 0, :],
                                       ALU.subtract).then_inc(xt_centred_pool, 1)
                for j in range(POOL_K):
                    k = DVE_K + j
                    pool.wait_ge(xt_centred_pool, b * POOL_K + (j + 1 - POOL_K))
                    pool.tensor_tensor(xt_f32[:, k, :], xt_f32[:, k, :], norm_rows[:, 1, :],
                                       ALU.mult).then_inc(xt_normed_pool, 1)

            for n in range(2 * TPB):
                rstd(norm_x, n, n % TPB)
            for d in range(KD):
                pool.wait_ge(wqkv_high, 2 * KD + d + 1)
                pool.tensor_tensor(wv[:, :, LOW, cols(d)], wqkv_raw[:, 2 * KD + d, :, :],
                                   wv[:, :, HIGH, cols(d)].bitcast(F32), ALU.subtract).then_inc(wv_low, 1)
            with pool.Fori(1, BLOCKS - 1) as b:
                norm_share(b)
                for i in range(TPB):
                    rstd(norm_x, b * TPB + (TPB + i), i)
            norm_share(BLOCKS - 1)
            with pool.Fori(0, TILES - 3) as t:
                rstd(norm_a, t, 0)
                sum_x1(t)
            rstd(norm_t, 0, 0)
            rstd(norm_t, 1, 1)
            rstd(norm_a, TILES - 3, 0)
            sum_x1(TILES - 3)
            rstd(norm_t, 2, 2)
            rstd(norm_t, 3, 3)
            for t in (TILES - 2, TILES - 1):
                rstd(norm_a, t, 0)
                sum_x1(t)

            def outputs(b):
                with pool.Fori(0, TPB) as i:
                    rstd(norm_y, b * TPB + i, 0)
                    sum_y(b, i)

            with pool.Fori(0, BLOCKS - 1) as b:
                for i in range(TPB):
                    rstd(norm_t, b * TPB + (TPB + i), i)
                outputs(b)
            for i in range(TPB):
                rstd(norm_y, (BLOCKS - 1) * TPB + i, i)

        @block.scalar
        def _(act):
            def split_wqkv(m):
                act.wait_ge(wqkv_loaded[m], 16)
                if m < 2 * KD:
                    dst = wqk[:, HIGH, :, cols(m)]
                else:
                    dst = wv[:, :, HIGH, cols(m - 2 * KD)]
                act.copy(dst, wqkv_raw[:, m, :, :]).then_inc(wqkv_high, 1)

            def xt_group(n, i, g):
                act.wait_ge(xt_ready, n * 2 + (g + 1))
                act.copy(xn_t[:, HIGH, 4 * g:4 * g + 4, cols(i)],
                         ps[:, 4 + 2 * (i % 2) + g, :].rearrange("p (k t) -> p k t", k=4)).then_inc(xt_high, 1)

            def xt_piece(n, i, g):
                if g == 0:
                    act.wait_ge(v_halfway, n + 1)
                else:
                    act.wait_ge(v_ready, n + 1)
                act.copy(xn_t[:, HIGH, 4 * g:4 * g + 4, cols(i)],
                         xt_f32[:, 4 * g:4 * g + 4, cols(i)]).then_inc(xt_high, 1)

            def qk_out(b):
                for m in range(2 * KD):
                    act.wait_ge(qk_ready, b * (2 * KD) + (m + 1))
                    d = m % KD
                    if m < KD:
                        act.activation(q_t[:, d, cols(b, BLOCK)], ps[:, m, :], ACT.Identity,
                                       bias=bqk_sb[:, m:m + 1]).then_inc(q_copied, 1)
                    else:
                        act.activation(k_t[:, d, HIGH, cols(b, BLOCK)], ps[:, m, :], ACT.Identity,
                                       bias=bqk_sb[:, m:m + 1]).then_inc(k_high, 1)

            def v_out(n, i):
                act.wait_ge(v_summed, n + 1)
                act.copy(v[:, n, HIGH, :], v_sum[:, i % 2, :]).then_inc(v_high, 1)

            for i in range(TPB):
                xt_group(i, i, 0)
                xt_group(i, i, 1)
                if i == 0:
                    split_wqkv(0)
            for m in range(1, WT):
                split_wqkv(m)
            act.wait_ge(bqk_loaded, 16)
            act.wait_ge(norm_x.stats_done, 2 * 2 * TPB)
            with act.Fori(0, BLOCKS - 1) as b:
                qk_out(b)
                act.wait_ge(xt_normed, b * DVE_K + DVE_K)
                for i in range(TPB):
                    xt_piece(b * TPB + i, i, 0)
                    if i == 0:
                        act.wait_ge(xt_normed_pool, b * POOL_K + POOL_K)
                    xt_piece(b * TPB + i, i, 1)
                for i in range(TPB):
                    v_out(b * TPB + i, i)
            act.wait_ge(wo_loaded, 16)
            act.wait_ge(xt_low, 2 * TILES)
            act.copy(wo_sb[:, HIGH, :, :], wo_raw[:]).then_inc(wo_high, 1)
            qk_out(BLOCKS - 1)

            def q_split(t):
                if type(t) is not int or t > 0:
                    act.wait_ge(s_ready, t * 4)
                else:
                    act.wait_ge(q_copied, KD * BLOCKS)
                act.copy(q_tile[:, HIGH, :, :], q_t[:, :, cols(t)]).then_inc(q_high, 1)

            def split_item_high(b, s, slot, pair=None):
                whole = not (type(s) is int and s in half_items)
                pair = s // 2 if pair is None else pair
                act.wait_ge(w_loaded[slot], b * (16 * ITEMS // 2) + pair * 16 + 16)
                n = ITEM // 2
                if whole:
                    for p in (0, 1):
                        act.copy(w_sb[:, slot, HIGH, p * n:(p + 1) * n], w_raw[:, slot, p * n:(p + 1) * n]).then_inc(w_high, 1)
                else:
                    act.copy(w_sb[:, slot, HIGH, 0:n], w_raw[:, slot, 0:n]).then_inc(w_high, 2)

            def ot_split(t):
                act.wait_ge(ot_ready, t + 1)
                act.copy(o_t[:, HIGH, :, :], ps[:, 7, 0:D].rearrange("p (k t) -> p k t", k=KD)).then_inc(ot_high, 1)

            def pt_split(t, g, bank):
                act.wait_ge(pt_ready, t * 4 + (g + 1))
                act.copy(probs_t[:, HIGH, 4 * g:4 * g + 4, :],
                         ps[:, bank, :].rearrange("p (k t) -> p k t", k=4)).then_inc(pt_high, 1)

            def exponentials(t):
                act.wait_ge(max_negated, t + 1)
                for g in range(4):
                    act.activation(probs[:, cols(g, BANK)], ps[:, g, :], ACT.Exp, bias=neg_max[:],
                                   scale=float(D) ** -0.5, accum_out=bank_sum[:, g:g + 1]).then_inc(exp_done, 1)

            def o_out(t):
                act.wait_ge(sum_inverted, t + 1)
                act.wait_ge(pv_ready, t + 1)
                act.activation(o_half[:], ps[:, 6, D:2 * D], ACT.Copy, scale=inv_sum[:]).then_inc(o_halved, 1)

            def attend(t, item=None):
                inner = type(t) is not int
                if inner or t >= 2:
                    ot_split(t - 2)
                for g in range(4):
                    pt_split(t - 1, g, 4 + g % 2)
                if inner or t < TILES - 1:
                    q_split(t + 1)
                exponentials(t)
                if item is not None:
                    split_item_high(0, item, item)
                o_out(t - 1)

            q_split(0)
            first = (BLOCKS - 1) * TPB
            v_out(first, 0)
            q_split(1)
            exponentials(0)
            for i in range(1, TPB):
                v_out(first + i, i)
            attend(1, 0)
            attend(2, 1)
            with act.Fori(3, TILES - 1) as t:
                attend(t)
            attend(TILES - 1)

            def x1t_tile(n, i):
                for g in (0, 1):
                    act.wait_ge(x1t_ready, n * 2 + (g + 1))
                    act.copy(x1n_t[:, HIGH, 4 * g:4 * g + 4, cols(i)],
                             ps[:, 2 * (i % 2) + g, :].rearrange("p (k t) -> p k t", k=4)).then_inc(x1t_high, 1)

            last = TILES - 1
            pt_split(last, 0, 0)
            pt_split(last, 1, 1)
            ot_split(last - 1)
            pt_split(last, 2, 2)
            pt_split(last, 3, 3)
            x1t_tile(0, 0)
            x1t_tile(1, 1)
            o_out(last)
            x1t_tile(2, 2)
            x1t_tile(3, 3)

            def tick(b, s, slot, pair=None):
                act.wait_ge(item_used, b * ITEMS + s)
                if type(s) is int and s == ITEMS - 1:
                    split_item_high(b + 1, 0, 0)
                else:
                    split_item_high(b, s + 1, 1 - slot, pair)

            def silu(b, c, slot):
                act.wait_ge(gate_ready, b * FULL + c + 1)
                if type(c) is not int or c > 0:
                    act.wait_ge(prod_done, b * UPS + c)
                act.activation(silu_sb[:, slot, :], ps[:, 2 * slot, :], ACT.Silu).then_inc(silu_done, 1)

            def silu_rest(b):
                act.wait_ge(item_used, b * ITEMS + 1)
                act.activation(silu_sb[REST:P, 0, :], ps[0:REST, 0, :], ACT.Silu).then_inc(silu_done, 1)

            def up(b, first):
                if first:
                    ot_split(TILES - 1)
                else:
                    tick(b, 0, 0)
                tick(b, 1, 1)
                silu_rest(b)
                with act.Fori(0, FULL // 2) as p:
                    tick(b, p * 2 + 2, 0, p + 1)
                    silu(b, p * 2, 1)
                    tick(b, p * 2 + 3, 1, p + 2)
                    silu(b, p * 2 + 1, 0)

            def y_out(i, half, bank):
                act.copy(y_tile[:, i, cols(half, BANK)], ps[:, bank, :]).then_inc(y_copied, 1)

            def down(b, more):
                for s in range(UPS, ITEMS):
                    if s < ITEMS - 1 or more:
                        tick(b, s, s % 2)
                    if s == UPS:
                        silu(b, FULL - 1, 1)
                    if more and UPS < s <= UPS + TPB:
                        x1t_tile(b * TPB + (s - UPS - 1 + TPB), s - UPS - 1)
                    if s == SHORT + 1:
                        act.wait_ge(stored, b * (16 * TPB) + 16 * TILES)
                        for i in range(TPB):
                            y_out(i, 0, TPB + i)
                for i in range(TPB):
                    if i < TPB - 1:
                        act.wait_ge(y_ready, b * (TPB - 1) + (i + 1))
                    else:
                        act.wait_ge(item_used, b * ITEMS + ITEMS)
                    y_out(i, 1, i)

            up(0, True)
            with act.Fori(0, BLOCKS - 1) as b:
                down(b, True)
                up(b + 1, False)
            down(BLOCKS - 1, False)

        @block.vector
        def _(dve):
            def row_stats(norm, i, src):
                for h in range(HALF):
                    dve.bn_stats(norm.stats[:, i, h, :], src[:, cols(h, BANK)]).then_inc(norm.stats_done, 1)

            def stats_in(norm, n):
                dve.wait_ge(norm.stats_done, n * 2 + 2)

            def moments(norm, i):
                dve.bn_aggr(norm.moments[:, :, i], norm.stats[:, i, :, :]).then_inc(norm.moments_done, 1)

            def normed(norm, n, i, src, done):
                dve.wait_ge(norm.rstd_done, n + 1)
                dve.tensor_scalar(src, src, norm.moments[:, 0, i:i + 1], norm.rstd[:, i:i + 1],
                                  ALU.subtract, ALU.mult).then_inc(done, 1)

            def low(dst, src, high):
                return dve.tensor_tensor(dst, src, high.bitcast(F32), ALU.subtract)

            def x_stats(i):
                dve.wait_ge(x_loaded[i - 1], 16)
                row_stats(norm_x, i, x_tile[:, i, :])

            def x_normed(n, i):
                normed(norm_x, n, i, x_tile[:, i, :], xn_done)

            def split_wqk(m):
                dve.wait_ge(wqkv_high, m + 1)
                low(wqk[:, LOW, :, cols(m)], wqkv_raw[:, m, :, :], wqk[:, HIGH, :, cols(m)]).then_inc(wqk_low, 1)

            def xt_group(n, i, g):
                dve.wait_ge(xt_high, n * 2 + (g + 1))
                k = slice(4 * g, 4 * g + 4)
                low(xn_t[:, LOW, k, cols(i)], ps[:, 4 + 2 * (i % 2) + g, :].rearrange("p (k t) -> p k t", k=4),
                    xn_t[:, HIGH, k, cols(i)]).then_inc(xt_low, 1)

            def centre(b, k):
                dve.tensor_tensor(xt_f32[:, k, :], xt_f32[:, k, :], norm_rows[:, 0, :],
                                  ALU.subtract).then_inc(xt_centred, 1)

            def scale(b, k):
                dve.wait_ge(xt_centred, b * DVE_K + (k + 1 - DVE_K))
                dve.tensor_tensor(xt_f32[:, k, :], xt_f32[:, k, :], norm_rows[:, 1, :],
                                  ALU.mult).then_inc(xt_normed, 1)

            def xt_piece(n, i, g):
                dve.wait_ge(xt_high, n * 2 + (g + 1))
                k = slice(4 * g, 4 * g + 4)
                low(xn_t[:, LOW, k, cols(i)], xt_f32[:, k, cols(i)], xn_t[:, HIGH, k, cols(i)]).then_inc(xt_low, 1)

            def k_split(b):
                for d in range(KD):
                    dve.wait_ge(k_high, b * KD + (d + 1))
                    m = KD + d
                    dve.scalar_tensor_tensor(out=k_t[:, d, LOW, cols(b, BLOCK)], in0=ps[:, m, :],
                                             scalar=bqk_sb[:, m:m + 1],
                                             in1=k_t[:, d, HIGH, cols(b, BLOCK)].bitcast(F32),
                                             op0=ALU.add, op1=ALU.subtract).then_inc(k_low, 1)

            def v_add(n, i):
                dve.wait_ge(v_ready, n + 1)
                bank = ps[:, 4 + i, :]
                dve.tensor_tensor(v_half[:], bank[:, D:2 * D], bv_sb[:], ALU.add).then_inc(v_halved, 1)
                dve.wait_ge(v_halved, n + 1)
                dve.tensor_tensor(v_sum[:, i % 2, :], bank[:, 0:D], v_half[:], ALU.add).then_inc(v_summed, 1)

            def v_split(n, i):
                dve.wait_ge(v_high, n + 1)
                low(v[:, n, LOW, :], v_sum[:, i % 2, :], v[:, n, HIGH, :]).then_inc(v_low, 1)

            def project(b, more):
                if more:
                    dve.wait_ge(rows_loaded, b * 16 + 16)
                    dve.wait_ge(norm_x.moments_done, b * TPB + 2 * TPB)
                    for i in range(TPB):
                        row_stats(norm_x, i, x_rows[:, i, :])
                    stats_in(norm_x, b * TPB + (3 * TPB - 1))
                dve.wait_ge(xt_loaded, b * 32 + 32)
                dve.wait_ge(norm_rows_loaded, b * 16 + 16)
                centre(b + 1, 0)
                if more:
                    for i in range(TPB):
                        moments(norm_x, i)
                for k in range(1, DVE_K):
                    centre(b + 1, k)
                for k in range(DVE_K):
                    scale(b + 1, k)
                for i in range(TPB):
                    xt_piece(b * TPB + (TPB + i), i, 0)
                    xt_piece(b * TPB + (TPB + i), i, 1)
                k_split(b)
                for i in range(TPB):
                    v_add(b * TPB + i, i)
                    v_split(b * TPB + i, i)

            for h in range(HALF):
                dve.wait_ge(x_half_loaded[h], 16)
                dve.bn_stats(norm_x.stats[:, 0, h, :], x_tile[:, 0, cols(h, BANK)]).then_inc(norm_x.stats_done, 1)
            stats_in(norm_x, 0)
            moments(norm_x, 0)

            def x_moments(i):
                x_stats(i)
                stats_in(norm_x, i)
                moments(norm_x, i)

            def both_groups(i):
                xt_group(i, i, 0)
                xt_group(i, i, 1)

            x_moments(1)
            x_normed(0, 0)
            x_moments(2)
            x_normed(1, 1)
            both_groups(0)
            x_normed(2, 2)
            split_wqk(0)
            both_groups(1)
            x_moments(3)
            both_groups(2)
            x_normed(3, 3)
            both_groups(3)
            split_wqk(1)
            dve.wait_ge(rows_first_loaded, 16)
            for i in range(TPB):
                row_stats(norm_x, i, rows_first[:, i, :])
                if i == TPB // 2:
                    split_wqk(2)
                stats_in(norm_x, TPB + i)
                moments(norm_x, i)
            split_wqk(3)
            dve.wait_ge(bqk_loaded, 16)
            dve.wait_ge(bv_loaded, 16)
            with dve.Fori(0, BLOCKS - 2) as b:
                project(b, True)
            project(BLOCKS - 2, False)
            dve.wait_ge(wo_high, 1)
            low(wo_sb[:, LOW, :, :], wo_raw[:], wo_sb[:, HIGH, :, :]).then_inc(wo_low, 1)
            k_split(BLOCKS - 1)

            def q_split(t):
                dve.wait_ge(q_high, t + 1)
                low(q_tile[:, LOW, :, :], q_t[:, :, cols(t)], q_tile[:, HIGH, :, :]).then_inc(q_low, 1)

            def split_item_low(b, s, slot):
                whole = not (type(s) is int and s in half_items)
                n = ITEM // 2
                for p in ((0, 1) if whole else (0,)):
                    dve.wait_ge(w_high, b * (2 * ITEMS) + s * 2 + (p + 1))
                    part = slice(p * n, (p + 1) * n)
                    low(w_sb[:, slot, LOW, part], w_raw[:, slot, part],
                        w_sb[:, slot, HIGH, part]).then_inc(w_low, 1 if whole else 2)

            def invert_sum(t):
                dve.wait_ge(exp_done, t * 4 + 4)
                dve.reduce_sum(row_sum[:], bank_sum[:], AX.X).then_inc(sum_done, 1)
                dve.wait_ge(sum_done, t + 1)
                dve.reciprocal(inv_sum[:], row_sum[:]).then_inc(sum_inverted, 1)

            def ot_split(t):
                dve.wait_ge(ot_high, t + 1)
                low(o_t[:, LOW, :, :], ps[:, 7, 0:D].rearrange("p (k t) -> p k t", k=KD),
                    o_t[:, HIGH, :, :]).then_inc(ot_low, 1)

            def maximum(t, g):
                dve.wait_ge(s_ready, t * 4 + (g + 1))
                dve.reduce_max(bank_max[:, g:g + 1], ps[:, g, :], AX.X).then_inc(bank_maxed, 1)
                if g == 3:
                    dve.wait_ge(bank_maxed, t * 4 + 4)
                    dve.reduce_max(row_max[:], bank_max[:], AX.X).then_inc(row_maxed, 1)
                    dve.wait_ge(row_maxed, t + 1)
                    dve.tensor_scalar(neg_max[:], row_max[:], -float(D) ** -0.5, None,
                                      ALU.mult).then_inc(max_negated, 1)

            def pt_split(t, g, bank):
                dve.wait_ge(pt_high, t * 4 + (g + 1))
                k = slice(4 * g, 4 * g + 4)
                low(probs_t[:, LOW, k, :], ps[:, bank, :].rearrange("p (k t) -> p k t", k=4),
                    probs_t[:, HIGH, k, :]).then_inc(pt_low, 1)

            def a_out(t, h):
                dve.wait_ge(a_ready, t * 2 + (h + 1))
                dve.tensor_tensor(x1_tile[:, cols(h, BANK)], ps[:, 4 + h, :], bo_sb[:, cols(h, BANK)],
                                  ALU.add).then_inc(a_copied, 1)

            def a_stats(t):
                dve.wait_ge(a_copied, t * 2 + 2)
                row_stats(norm_a, 0, x1_tile)
                stats_in(norm_a, t)

            def o_out(t):
                dve.wait_ge(o_halved, t + 1)
                dve.scalar_tensor_tensor(out=o_sum[:], in0=ps[:, 6, 0:D], scalar=inv_sum[:], in1=o_half[:],
                                         op0=ALU.mult, op1=ALU.add).then_inc(o_ready, 1)

            def a_norm(t):
                normed(norm_a, t, 0, x1_tile[:], a_normed)

            def t_stats(b, i):
                dve.wait_ge(t_loaded[i], b * 16 + 16)
                row_stats(norm_t, i, t_tile[:, i, :])

            def t_normed(b, i):
                normed(norm_t, b * TPB + i, i, t_tile[:, i, :], x1n_done)

            def first_block_moments(i):
                t_stats(0, i)
                stats_in(norm_t, i)
                moments(norm_t, i)

            def attend(t, item=None):
                inner = type(t) is not int
                invert_sum(t - 1)
                if inner or t >= 2:
                    ot_split(t - 2)
                for g in range(4):
                    maximum(t, g)
                    pt_split(t - 1, g, 4 + g % 2)
                if not inner and t < TILES - 1:
                    q_split(t + 1)
                if t is last:
                    first_block_moments(0)
                    first_block_moments(1)
                    t_normed(0, 0)
                if inner or t >= 2:
                    dve.wait_ge(x_res_loaded, t * 16 - 16)
                    a_out(t - 2, 0)
                    a_out(t - 2, 1)
                    a_stats(t - 2)
                    if inner:
                        q_split(t + 1)
                    moments(norm_a, 0)
                if item is not None:
                    split_item_low(0, item, item)
                o_out(t - 1)
                if inner or 2 <= t < last:
                    a_norm(t - 2)

            last = TILES - 1
            first = (BLOCKS - 1) * TPB
            q_split(0)
            v_add(first, 0)
            v_split(first, 0)
            for g in range(4):
                maximum(0, g)
            q_split(1)
            for i in range(1, TPB):
                v_add(first + i, i)
                v_split(first + i, i)
            attend(1, 0)
            dve.wait_ge(bo_loaded, 16)
            attend(2, 1)
            with dve.Fori(3, TILES - 1) as t:
                attend(t)
            attend(last)

            def x1t_tile(n, i):
                for g in (0, 1):
                    dve.wait_ge(x1t_high, n * 2 + (g + 1))
                    k = slice(4 * g, 4 * g + 4)
                    low(x1n_t[:, LOW, k, cols(i)], ps[:, 2 * (i % 2) + g, :].rearrange("p (k t) -> p k t", k=4),
                        x1n_t[:, HIGH, k, cols(i)]).then_inc(x1t_low, 1)

            def t_stats_in(b, i):
                stats_in(norm_t, b * TPB + i)

            def t_pair(b, i):
                t_stats(b, i)
                t_stats_in(b, i)
                t_stats(b, i + 1)
                moments(norm_t, i)
                t_normed(b, i)

            def t_second(b, i):
                moments(norm_t, i)
                t_normed(b, i)

            invert_sum(last)
            pt_split(last, 0, 0)
            a_norm(last - 2)
            pt_split(last, 1, 1)
            ot_split(last - 1)
            pt_split(last, 2, 2)
            pt_split(last, 3, 3)
            t_normed(0, 1)
            first_block_moments(2)
            first_block_moments(3)
            t_normed(0, 2)
            t_normed(0, 3)
            x1t_tile(0, 0)
            x1t_tile(1, 1)
            o_out(last)
            x1t_tile(2, 2)
            x1t_tile(3, 3)
            dve.wait_ge(x_res_loaded, last * 16)
            a_out(last - 1, 0)
            a_out(last - 1, 1)
            a_stats(last - 1)
            moments(norm_a, 0)
            a_norm(last - 1)

            def tick(b, s, slot):
                if type(s) is int and s == ITEMS - 1:
                    split_item_low(b + 1, 0, 0)
                else:
                    split_item_low(b, s + 1, 1 - slot)

            def hidden(b, c, slot):
                dve.wait_ge(h_low, b * UPS + c + 1)
                dve.wait_ge(silu_done, b * UPS + c + 2)
                dve.wait_ge(item_used, b * ITEMS + c + 2)
                dve.tensor_tensor(h_f32[:], silu_sb[:, slot, :], ps[:, 2 * slot + 1, :], ALU.mult).then_inc(prod_done, 1)
                dve.wait_ge(prod_done, b * UPS + c + 2)
                dve.tensor_copy(h_t[:, c, HIGH, :], h_f32[:]).then_inc(h_high, 1)
                dve.wait_ge(h_high, b * UPS + c + 2)
                low(h_t[:, c, LOW, :], h_f32[:], h_t[:, c, HIGH, :]).then_inc(h_low, 1)

            def hidden_rest(b):
                up_half = slice(REST, P)
                dve.wait_ge(silu_done, b * UPS + 1)
                dve.tensor_tensor(h_f32[up_half, :], silu_sb[up_half, 0, :], ps[up_half, 0, :],
                                  ALU.mult).then_inc(prod_done, 1)
                dve.wait_ge(prod_done, b * UPS + 1)
                dve.tensor_copy(h_rest[0:REST, :], h_f32[up_half, :])
                dve.tensor_copy(h_rest[up_half, :], h_f32[up_half, :]).then_inc(h_high, 1)
                dve.wait_ge(h_high, b * UPS + 1)
                low(h_rest[up_half, :], h_f32[up_half, :], h_rest[up_half, :]).then_inc(h_low, 1)

            def y_stats(b, i):
                dve.wait_ge(y_copied, b * (2 * TPB) + i + (TPB + 1))
                row_stats(norm_y, 0, y_tile[:, i, :])

            def y_norm(b, i):
                normed(norm_y, b * TPB + i, 0, y_tile[:, i, :], y_normed)

            def up(b, post):
                if post is None:
                    ot_split(last)
                else:
                    tick(b, 0, 0)
                tick(b, 1, 1)
                hidden_rest(b)
                if post is None:
                    dve.wait_ge(x_res_loaded, TILES * 16)
                    a_out(last, 0)
                    a_out(last, 1)
                    a_stats(last)
                    moments(norm_a, 0)
                    a_norm(last)
                else:
                    with dve.Fori(0, TPB) as i:
                        tick(b, i * 2 + 2, 0)
                        hidden(b, i * 2, 1)
                        y_stats(post, i)
                        stats_in(norm_y, post * TPB + i)
                        tick(b, i * 2 + 3, 1)
                        moments(norm_y, 0)
                        hidden(b, i * 2 + 1, 0)
                        y_norm(post, i)
                with dve.Fori(0 if post is None else TPB, FULL // 2) as p:
                    tick(b, p * 2 + 2, 0)
                    hidden(b, p * 2, 1)
                    tick(b, p * 2 + 3, 1)
                    hidden(b, p * 2 + 1, 0)

            def down(b, more):
                for s in range(UPS, ITEMS):
                    if more and s in (UPS + 1, UPS + 3):
                        t_stats_in(b + 1, s - UPS)
                    if s < ITEMS - 1 or more:
                        tick(b, s, s % 2)
                    if s == UPS:
                        hidden(b, FULL - 1, 1)
                    if more and s in (UPS, UPS + 2):
                        t_pair(b + 1, s - UPS)
                    if more and s in (UPS + 1, UPS + 3):
                        t_second(b + 1, s - UPS)
                    if more and UPS < s <= UPS + TPB:
                        x1t_tile(b * TPB + (s - UPS - 1 + TPB), s - UPS - 1)
                    if not more and s == ITEMS - 2:
                        dve.wait_ge(y_copied, b * (2 * TPB) + TPB)
                        for i in range(TPB):
                            dve.bn_stats(norm_y.stats[:, i, 0, :], y_tile[:, i, 0:BANK]).then_inc(norm_y.stats_done, 1)

            up(0, None)
            with dve.Fori(0, BLOCKS - 1) as b:
                down(b, True)
                up(b + 1, b)
            down(BLOCKS - 1, False)
            b = BLOCKS - 1

            def last_moments(i):
                dve.wait_ge(y_copied, b * (2 * TPB) + TPB + i + 1)
                dve.bn_stats(norm_y.stats[:, i, 1, :], y_tile[:, i, BANK:C]).then_inc(norm_y.stats_done, 1)
                dve.wait_ge(norm_y.stats_done, b * (2 * TPB) + TPB + i + 1)
                moments(norm_y, i)

            def last_normed(i, part):
                dve.wait_ge(norm_y.rstd_done, b * TPB + i + 1)
                dve.tensor_scalar(y_tile[:, i, part], y_tile[:, i, part], norm_y.moments[:, 0, i:i + 1],
                                  norm_y.rstd[:, i:i + 1], ALU.subtract, ALU.mult).then_inc(y_normed, 1)

            def last_sum(i, part, done):
                dve.wait_ge(y_normed, b * TPB + done)
                dve.tensor_tensor(y_tile[:, i, part], y_tile[:, i, part], t_tile[:, i, part],
                                  ALU.add).then_inc(y_added, 1)

            whole = slice(0, C)
            dve.wait_ge(r_loaded, BLOCKS * 16 * TPB)
            for i in range(TPB):
                last_moments(i)
                if i > 0:
                    last_sum(i - 1, whole, i)
                if i < TPB - 1:
                    last_normed(i, whole)
            for h in range(HALF):
                last_normed(TPB - 1, cols(h, BANK))
            for h in range(HALF):
                last_sum(TPB - 1, cols(h, BANK), TPB + h)

        @block.tensor
        def _(pe):
            pe.wait_ge(ident_ready, 1)

            def transposes(bank, k0, src, count):
                for j in range(count):
                    last = pe.transpose(ps[:, bank, cols(j)], src[:, cols(k0 + j)], ident[:])
                return last

            def xt_group(i, g):
                if g == 0:
                    pe.wait_ge(xn_done, i + 1)
                if i > 1:
                    pe.wait_ge(xt_low, i * 2 + (g - 3))
                transposes(4 + 2 * (i % 2) + g, 4 * g, x_tile[:, i, :], 4).then_inc(xt_ready, 1)

            def qk_piece(m, b=None):
                if b is not None and m >= KD:
                    pe.wait_ge(k_low, b * KD + (m + 1 - 2 * KD))
                pe.wait_ge(wqk_low, m + 1)
                for k in range(KC):
                    last = three(pe, ps[:, m, :], lambda p: wqk[:, p, k, cols(m)], lambda p: xn_t[:, p, k, :],
                                 k == 0, k == KC - 1)
                last.then_inc(qk_ready, 1)

            def qk(b):
                for k in range(KC):
                    if k % 4 == 0:
                        pe.wait_ge(xt_low, b * (2 * TPB) + (2 * TPB - 1 + k // 4))
                    last = three(pe, ps[:, 0, :], lambda p: wqk[:, p, k, cols(0)], lambda p: xn_t[:, p, k, :],
                                 k == 0, k == KC - 1)
                last.then_inc(qk_ready, 1)
                for m in range(1, 2 * KD):
                    qk_piece(m, b)

            def first_piece(h, g):
                for k in range(4 * g, 4 * g + 4):
                    last = three(pe, ps[:, 0, cols(h, BLOCK // 2)], lambda p: wqk[:, p, k, cols(0)],
                                 lambda p: xn_t[:, p, k, cols(h, BLOCK // 2)], k == 0, k == KC - 1)
                return last

            def project_v(b, i):
                bank = ps[:, 4 + i, :]
                if type(b) is int:
                    pe.wait_ge(v_summed, (b - 1) * TPB + i + 1)
                elif i == 0:
                    pe.wait_ge(xt_centred, b * DVE_K + 1)
                for k in range(KC):
                    pe.matmul(bank, xn_t[:, HIGH, k, cols(i)], wv[:, k, :, :], start=k == 0, stop=False)
                    last = pe.matmul(bank[:, 0:D], xn_t[:, LOW, k, cols(i)], wv[:, k, HIGH, :],
                                     start=False, stop=k == KC - 1)
                    if k == KC // 2 - 1:
                        last.then_inc(v_halfway, 1)
                last.then_inc(v_ready, 1)

            for i in range(TPB - 1):
                xt_group(i, 0)
                xt_group(i, 1)
            pe.wait_ge(wqk_low, 1)
            pe.wait_ge(xt_low, TPB)
            for g in (0, 1):
                first_piece(0, g)
            for g in (0, 1):
                xt_group(TPB - 1, g)
            for g in (0, 1):
                pe.wait_ge(xt_low, 2 * TPB - 1 + g)
                last = first_piece(1, g)
            last.then_inc(qk_ready, 1)
            for m in range(1, 2 * KD):
                qk_piece(m)
            with pe.Fori(0, BLOCKS - 1) as b:
                pe.wait_ge(wv_low, KD)
                for i in range(TPB):
                    project_v(b, i)
                qk(b + 1)

            def scores(t, g):
                for d in range(KD):
                    last = three(pe, ps[:, g, :], lambda p: q_tile[:, p, d, :],
                                 lambda p: k_t[:, d, p, cols(g, BANK)], d == 0, d == KD - 1)
                last.then_inc(s_ready, 1)

            def transpose_probs(g, bank):
                transposes(bank, 4 * g, probs, 4).then_inc(pt_ready, 1)

            def transpose_output(t):
                pe.wait_ge(o_ready, t + 1)
                transposes(7, 0, o_sum, KD).then_inc(ot_ready, 1)

            def project_output(h):
                for d in range(KD):
                    last = three(pe, ps[:, 4 + h, :], lambda p: o_t[:, p, d, :],
                                 lambda p: wo_sb[:, p, d, cols(h, BANK)], d == 0, d == KD - 1)
                last.then_inc(a_ready, 1)

            def weigh(t, g):
                pe.wait_ge(pt_low, t * 4 + (g + 1))
                for k in range(4 * g, 4 * g + 4):
                    pe.matmul(ps[:, 6, :], probs_t[:, HIGH, k, :], v[:, k, :, :], start=k == 0, stop=False)
                    last = pe.matmul(ps[:, 6, 0:D], probs_t[:, LOW, k, :], v[:, k, HIGH, :],
                                     start=False, stop=k == TILES - 1)
                if g == 3:
                    last.then_inc(pv_ready, 1)

            def attend(t):
                older = type(t) is not int or t >= 2
                pe.wait_ge(q_low, t + 1)
                for g in range(4):
                    pe.wait_ge(exp_done, t * 4 + (g - 3))
                    scores(t, g)
                    if older and g == 0:
                        transpose_output(t - 2)
                    if g > 1:
                        pe.wait_ge(pt_low, t * 4 + (g - 5))
                    elif not older:
                        pe.wait_ge(v_summed, TILES - TPB + 1 + g)
                    transpose_probs(g, 4 + g % 2)
                if older:
                    pe.wait_ge(ot_low, t - 1)
                else:
                    pe.wait_ge(v_low, TILES)
                for g in range(4):
                    if older and g < HALF:
                        pe.wait_ge(pt_low, t * 4 + (g - 1))
                        project_output(g)
                    weigh(t - 1, g)

            project_v(BLOCKS - 1, 0)
            pe.wait_ge(k_low, KD * BLOCKS)
            pe.wait_ge(q_low, 1)
            for g in range(4):
                scores(0, g)
            for i in range(1, TPB):
                project_v(BLOCKS - 1, i)
            attend(1)
            pe.wait_ge(wo_low, 1)
            with pe.Fori(2, TILES) as t:
                attend(t)

            def x1t_tile(n, i):
                pe.wait_ge(x1n_done, n + 1)
                for g in (0, 1):
                    if i > 1:
                        pe.wait_ge(x1t_low, n * 2 + (g - 3))
                    transposes(2 * (i % 2) + g, 4 * g, t_tile[:, i, :], 4).then_inc(x1t_ready, 1)

            last_tile = TILES - 1
            for g in range(4):
                pe.wait_ge(exp_done, 4 * last_tile + 4)
                transpose_probs(g, g)
                if g == 1:
                    transpose_output(last_tile - 1)
            for g in range(4):
                weigh(last_tile, g)
            x1t_tile(0, 0)
            x1t_tile(1, 1)
            pe.wait_ge(ot_low, last_tile)
            project_output(0)
            x1t_tile(2, 2)
            x1t_tile(3, 3)
            project_output(1)

            def up(b, post):
                if post is not None:
                    pe.wait_ge(y_copied, post * (2 * TPB) + (TPB + 1))
                pe.wait_ge(w_low, b * (2 * ITEMS) + 2)
                for k in range(KC):
                    if k % 4 == 0:
                        pe.wait_ge(x1t_low, b * (2 * TPB) + (2 * TPB - 1 + k // 4))
                    last = three(pe, ps[:, 0, :], lambda p: w_sb[:, 0, p, cols(k)], lambda p: x1n_t[:, p, k, :],
                                 k == 0, k == KC - 1)
                last.then_inc(item_used, 1)
                if post is None:
                    transpose_output(last_tile)

                def gate_up(c, slot, older):
                    if older:
                        pe.wait_ge(prod_done, b * UPS + c)
                    for part in (0, 1):
                        pe.wait_ge(w_low, b * (2 * ITEMS) + c * 2 + (part + 3))
                        for k in range(KC):
                            last = three(pe, ps[:, 2 * slot + part, :],
                                         lambda p: w_sb[:, slot, p, cols(part * KC + k)],
                                         lambda p: x1n_t[:, p, k, :], k == 0, k == KC - 1)
                        last.then_inc(item_used if part else gate_ready, 1)

                if post is not None:
                    pe.wait_ge(y_copied, post * (2 * TPB) + 2 * TPB)
                gate_up(0, 1, False)
                if post is None:
                    pe.wait_ge(ot_low, TILES)
                    pe.wait_ge(a_copied, HALF * last_tile)
                    project_output(0)
                    project_output(1)
                with pe.Fori(0, FULL // 2) as p:
                    gate_up(p * 2 + 1, 0, True)
                    gate_up(p * 2 + 2, 1, True)

            def down(b, more):
                def add_chunk(bank, i, c, w, first):
                    return three(pe, ps[:, bank, :], lambda p: h_t[:, c, p, cols(i)], w, first, False)

                def full_item(s, j, bank0, first, last):
                    slot = s % 2
                    pe.wait_ge(w_low, b * (2 * ITEMS) + (2 * s + 2))
                    for i in range(TPB):
                        for q in range(CPI):
                            c = CPI * j + q
                            mm = three(pe, ps[:, bank0 + i, :], lambda p: h_t[:, c, p, cols(i)],
                                       lambda p: w_sb[:, slot, p, cols(q, BANK)],
                                       first and q == 0, last and q == CPI - 1)
                        if last and i < TPB - 1:
                            mm.then_inc(y_ready, 1)
                    mm.then_inc(item_used, 1)

                def short_item(s, bank0, first, last):
                    slot = s % 2
                    pe.wait_ge(w_low, b * (2 * ITEMS) + (2 * s + 2))
                    for i in range(TPB):
                        three(pe, ps[:, bank0 + i, :], lambda p: h_t[:, FULL - 1, p, cols(i)],
                              lambda p: w_sb[:, slot, p, cols(0, BANK)], first, False)
                        for p in (HIGH, LOW):
                            mm = pe.matmul(ps[:, bank0 + i, :], h_rest[:, cols(i)], w_sb[:, slot, p, cols(1, BANK)],
                                           start=False, stop=last and p == LOW)
                    mm.then_inc(item_used, 1)

                for j in range(DOWN):
                    if more and j > 0:
                        if j == 1:
                            pe.wait_ge(prod_done, b * UPS + UPS)
                        x1t_tile(b * TPB + (TPB + j - 1), j - 1)
                    pe.wait_ge(h_low, b * UPS + (CPI * (j + 1) + 1))
                    full_item(UPS + j, j, TPB, j == 0, False)
                pe.wait_ge(h_low, b * UPS + UPS)
                short_item(SHORT, TPB, False, True)
                if more:
                    pe.wait_ge(x1t_low, b * (2 * TPB) + 4 * TPB)
                short_item(SHORT + 1, 0, True, False)
                for j in range(DOWN):
                    full_item(SHORT + 2 + j, j, 0, False, j == DOWN - 1)

            up(0, None)
            with pe.Fori(0, BLOCKS - 1) as b:
                down(b, True)
                up(b + 1, b)
            down(BLOCKS - 1, False)


def kernel(**inputs):
    import numpy as np
    import concourse.bacc as bacc
    from concourse.bass_utils import run_bass_kernel_spmd

    def chunks(a):
        return a.reshape(a.shape[0] // P, P, a.shape[1]).transpose(1, 0, 2)

    a = {name: np.asarray(value) for name, value in inputs.items()}
    bqkv = a["L0_attn_bqkv"]
    gate, up, down = a["L0_ffn_W_gate"].T, a["L0_ffn_W_up"].T, a["L0_ffn_W_down"].T
    short = UPS + DOWN
    wffn = np.zeros((ITEMS, P, ITEM), a["L0_ffn_W_gate"].dtype)
    wffn[0, :, 0:KC * P] = chunks(np.concatenate([gate[:, FULL * P:], up[:, FULL * P:]], 1)).reshape(P, -1)
    for c in range(FULL):
        f = slice(c * P, (c + 1) * P)
        wffn[1 + c, :, 0:KC * P] = chunks(gate[:, f]).reshape(P, -1)
        wffn[1 + c, :, KC * P:] = chunks(up[:, f]).reshape(P, -1)
    for h in range(HALF):
        part = down[:, h * BANK:(h + 1) * BANK]
        first = short + 2 if h else UPS
        for j in range(DOWN):
            wffn[first + j] = chunks(part[j * CPI * P:(j + 1) * CPI * P]).reshape(P, -1)
        wffn[short + h, :, 0:BANK] = part[(FULL - 1) * P:FULL * P]
        wffn[short + h, 0:REST, BANK:2 * BANK] = part[FULL * P:]
        wffn[short + h, REST:P, BANK:2 * BANK] = part[FULL * P:]

    arrays = {
        "x": a["L0_attn_x"].reshape(S, C),
        "xt": a["L0_attn_x"].reshape(BLOCKS, BLOCK, KC, P).transpose(0, 3, 2, 1),
        "wqkv": np.stack([chunks(a["L0_attn_Wqkv"][:, m * P:(m + 1) * P]) for m in range(WT)]),
        "bqk": bqkv[0:2 * D].reshape(2 * KD, P).T,
        "bv": np.broadcast_to(bqkv[2 * D:], (P, D)),
        "wo": chunks(a["L0_attn_Wo"]),
        "bo": np.broadcast_to(a["L0_attn_bo"], (P, C)),
        "wffn": wffn,
    }
    arrays = {name: np.ascontiguousarray(value) for name, value in arrays.items()}
    nc = bacc.Bacc("TRN2", target_bir_lowering=False, num_devices=1)
    args = [nc.dram_tensor(name, value.shape, mybir.dt.from_np(value.dtype), kind="ExternalInput").ap()
            for name, value in arrays.items()]
    args.append(nc.dram_tensor("out", (S, C), F32, kind="ExternalOutput").ap())
    transformer_block(nc, *args)
    result = run_bass_kernel_spmd(nc, [arrays], core_ids=[0])
    return result.results[0]["out"].reshape(a["L0_attn_x"].shape)
```
